# Optimizing a Trainium2 kernel written in Bass

```python
import numpy as np
import jax
import jax.numpy as jnp

def _softmax(x, axis=-1):
    return jax.nn.softmax(x, axis=axis)

def _gelu(x):
    return jax.nn.gelu(x, approximate=True)

def _silu(x):
    return jax.nn.silu(x)

def _sigmoid(x):
    return jax.nn.sigmoid(x)

def _layernorm(x, axis=-1, eps=1e-05):
    m = jnp.mean(x, axis=axis, keepdims=True)
    v = jnp.var(x, axis=axis, keepdims=True)
    return (x - m) / jnp.sqrt(v + eps)

def _scatter_add(tgt, idx, src, axis=0):
    return tgt.at[idx].add(src)

def _segment_sum(src, seg, n):
    return jax.ops.segment_sum(src, seg, n)
kernel_name = 'mk_prb_d1_jaxref_r4_42e5b3'

def setup_inputs(seed: int=0):
    np.random.seed(seed)
    _w = jnp.asarray

    def _L0_attn_setup():
        import jax, jax.numpy as jnp
        import numpy as np
        D_MODEL, D_STATE, D_CONV = (256, 16, 4)
        B_, L_ = (4, 512)
        LN_EPS = 1e-05

        def _silu(v):
            return v * jax.nn.sigmoid(v)

        def _mamba_fwd(x, in_proj_w, in_proj_b, conv_w, conv_b, bc_w, bc_b, dt_w, dt_b, A_log, D, out_w, out_b, ln_g, ln_b):
            b, l, d = x.shape
            x_proj = x @ in_proj_w.T + in_proj_b
            x_ssm, x_gate = jnp.split(x_proj, 2, axis=-1)
            xc = lax.conv_general_dilated(x_ssm.transpose(0, 2, 1), conv_w, window_strides=(1,), padding=[(D_CONV - 1, 0)], feature_group_count=d, dimension_numbers=('NCH', 'OIH', 'NCH'))
            x_conv = _silu((xc + conv_b[None, :, None]).transpose(0, 2, 1))
            BC = x_conv @ bc_w.T + bc_b
            Bm, Cm = jnp.split(BC, 2, axis=-1)
            dt = jax.nn.softplus(x_conv @ dt_w.T + dt_b)
            A = -jnp.exp(A_log)

            def step(h, inp):
                xt, dtt, Bt, Ct = inp
                dA = jnp.exp(dtt[:, :, None] * A)
                dB = dtt[:, :, None] * Bt[:, None, :]
                h = h * dA + dB * xt[:, :, None]
                y = jnp.einsum('bdn,bn->bd', h, Ct) + xt * D
                return (h, y)
            h0 = jnp.zeros((b, d, D_STATE), x.dtype)
            xs = (x_conv.transpose(1, 0, 2), dt.transpose(1, 0, 2), Bm.transpose(1, 0, 2), Cm.transpose(1, 0, 2))
            _, ys = lax.scan(step, h0, xs)
            y = ys.transpose(1, 0, 2)
            y = y * _silu(x_gate)
            out = y @ out_w.T + out_b
            z = out + x
            mu = jnp.mean(z, axis=-1, keepdims=True)
            var = jnp.var(z, axis=-1, keepdims=True)
            return (z - mu) * jax.lax.rsqrt(var + LN_EPS) * ln_g + ln_b
        from jax import lax
        key = jax.random.key(seed)
        ks = jax.random.split(key, 16)
        s = 0.02
        return {'x': jax.random.normal(ks[0], (B_, L_, D_MODEL), jnp.float32), 'in_proj_w': jax.random.normal(ks[1], (2 * D_MODEL, D_MODEL), jnp.float32) * s, 'in_proj_b': jnp.zeros((2 * D_MODEL,), jnp.float32), 'conv_w': jax.random.normal(ks[2], (D_MODEL, 1, D_CONV), jnp.float32) * s, 'conv_b': jnp.zeros((D_MODEL,), jnp.float32), 'bc_w': jax.random.normal(ks[3], (2 * D_STATE, D_MODEL), jnp.float32) * s, 'bc_b': jnp.zeros((2 * D_STATE,), jnp.float32), 'dt_w': jax.random.normal(ks[4], (D_MODEL, D_MODEL), jnp.float32) * s, 'dt_b': jnp.zeros((D_MODEL,), jnp.float32), 'A_log': jax.random.normal(ks[5], (D_MODEL, D_STATE), jnp.float32), 'D': jnp.ones((D_MODEL,), jnp.float32), 'out_w': jax.random.normal(ks[6], (D_MODEL, D_MODEL), jnp.float32) * s, 'out_b': jnp.zeros((D_MODEL,), jnp.float32), 'ln_g': jnp.ones((D_MODEL,), jnp.float32), 'ln_b': jnp.zeros((D_MODEL,), jnp.float32)}
    _L0_attn_in = _L0_attn_setup()

    def _L0_ffn_setup():
        import jax, jax.numpy as jnp
        import numpy as np
        B, T, D, E, H, K = (2, 512, 256, 8, 1024, 2)
        key = jax.random.key(seed)
        ks = jax.random.split(key, 8)
        s = 0.02
        return {'x': jax.random.normal(ks[0], (B, T, D), jnp.float32), 'rw1': jax.random.normal(ks[1], (D, D), jnp.float32) * s, 'rb1': jnp.zeros((D,), jnp.float32), 'rw2': jax.random.normal(ks[2], (D, E), jnp.float32) * s, 'rb2': jnp.zeros((E,), jnp.float32), 'we1': jax.random.normal(ks[3], (E, D, H), jnp.float32) * s, 'be1': jnp.zeros((E, H), jnp.float32), 'we2': jax.random.normal(ks[4], (E, H, D), jnp.float32) * s, 'be2': jnp.zeros((E, D), jnp.float32)}
    _L0_ffn_in = _L0_ffn_setup()
    _d = {'L0_attn_x': _L0_attn_in['x'], 'L0_attn_in_proj_w': _L0_attn_in['in_proj_w'], 'L0_attn_in_proj_b': _L0_attn_in['in_proj_b'], 'L0_attn_conv_w': _L0_attn_in['conv_w'], 'L0_attn_conv_b': _L0_attn_in['conv_b'], 'L0_attn_bc_w': _L0_attn_in['bc_w'], 'L0_attn_bc_b': _L0_attn_in['bc_b'], 'L0_attn_dt_w': _L0_attn_in['dt_w'], 'L0_attn_dt_b': _L0_attn_in['dt_b'], 'L0_attn_A_log': _L0_attn_in['A_log'], 'L0_attn_D': _L0_attn_in['D'], 'L0_attn_out_w': _L0_attn_in['out_w'], 'L0_attn_out_b': _L0_attn_in['out_b'], 'L0_attn_ln_g': _L0_attn_in['ln_g'], 'L0_attn_ln_b': _L0_attn_in['ln_b'], 'L0_ffn_rw1': _L0_ffn_in['rw1'], 'L0_ffn_rb1': _L0_ffn_in['rb1'], 'L0_ffn_rw2': _L0_ffn_in['rw2'], 'L0_ffn_rb2': _L0_ffn_in['rb2'], 'L0_ffn_we1': _L0_ffn_in['we1'], 'L0_ffn_be1': _L0_ffn_in['be1'], 'L0_ffn_we2': _L0_ffn_in['we2'], 'L0_ffn_be2': _L0_ffn_in['be2']}
    _x0 = _d['L0_attn_x']
    _d['L0_attn_x'] = jax.random.normal(jax.random.fold_in(jax.random.key(seed), 1), (8, 512, 256), dtype=_x0.dtype)
    del _x0
    return _d

def reference(L0_attn_x, L0_attn_in_proj_w, L0_attn_in_proj_b, L0_attn_conv_w, L0_attn_conv_b, L0_attn_bc_w, L0_attn_bc_b, L0_attn_dt_w, L0_attn_dt_b, L0_attn_A_log, L0_attn_D, L0_attn_out_w, L0_attn_out_b, L0_attn_ln_g, L0_attn_ln_b, L0_ffn_rw1, L0_ffn_rb1, L0_ffn_rw2, L0_ffn_rb2, L0_ffn_we1, L0_ffn_be1, L0_ffn_we2, L0_ffn_be2):

    def _L0_attn_ref(x, in_proj_w, in_proj_b, conv_w, conv_b, bc_w, bc_b, dt_w, dt_b, A_log, D, out_w, out_b, ln_g, ln_b):
        import jax, jax.numpy as jnp
        import numpy as np
        D_MODEL, D_STATE, D_CONV = (256, 16, 4)
        B_, L_ = (4, 512)
        LN_EPS = 1e-05

        def _silu(v):
            return v * jax.nn.sigmoid(v)

        def _mamba_fwd(x, in_proj_w, in_proj_b, conv_w, conv_b, bc_w, bc_b, dt_w, dt_b, A_log, D, out_w, out_b, ln_g, ln_b):
            b, l, d = x.shape
            x_proj = x @ in_proj_w.T + in_proj_b
            x_ssm, x_gate = jnp.split(x_proj, 2, axis=-1)
            xc = lax.conv_general_dilated(x_ssm.transpose(0, 2, 1), conv_w, window_strides=(1,), padding=[(D_CONV - 1, 0)], feature_group_count=d, dimension_numbers=('NCH', 'OIH', 'NCH'))
            x_conv = _silu((xc + conv_b[None, :, None]).transpose(0, 2, 1))
            BC = x_conv @ bc_w.T + bc_b
            Bm, Cm = jnp.split(BC, 2, axis=-1)
            dt = jax.nn.softplus(x_conv @ dt_w.T + dt_b)
            A = -jnp.exp(A_log)

            def step(h, inp):
                xt, dtt, Bt, Ct = inp
                dA = jnp.exp(dtt[:, :, None] * A)
                dB = dtt[:, :, None] * Bt[:, None, :]
                h = h * dA + dB * xt[:, :, None]
                y = jnp.einsum('bdn,bn->bd', h, Ct) + xt * D
                return (h, y)
            h0 = jnp.zeros((b, d, D_STATE), x.dtype)
            xs = (x_conv.transpose(1, 0, 2), dt.transpose(1, 0, 2), Bm.transpose(1, 0, 2), Cm.transpose(1, 0, 2))
            _, ys = lax.scan(step, h0, xs)
            y = ys.transpose(1, 0, 2)
            y = y * _silu(x_gate)
            out = y @ out_w.T + out_b
            z = out + x
            mu = jnp.mean(z, axis=-1, keepdims=True)
            var = jnp.var(z, axis=-1, keepdims=True)
            return (z - mu) * jax.lax.rsqrt(var + LN_EPS) * ln_g + ln_b
        from jax import lax
        return _mamba_fwd(x, in_proj_w, in_proj_b, conv_w, conv_b, bc_w, bc_b, dt_w, dt_b, A_log, D, out_w, out_b, ln_g, ln_b)

    def _L0_ffn_ref(x, rw1, rb1, rw2, rb2, we1, be1, we2, be2):
        import jax, jax.numpy as jnp
        import numpy as np
        B, T, D, E, H, K = (2, 512, 256, 8, 1024, 2)
        b, t, d = x.shape
        xt = x.reshape(b * t, d)
        n = xt.shape[0]
        logits = jax.nn.silu(xt @ rw1 + rb1) @ rw2 + rb2
        _, idx = jax.lax.top_k(logits, K)
        mask = jnp.zeros((n, E), bool).at[jnp.arange(n)[:, None], idx].set(True)
        w = jax.nn.softmax(jnp.where(mask, logits, -jnp.inf), axis=1)
        h = jax.nn.silu(jnp.einsum('nd,edh->enh', xt, we1) + be1[:, None, :])
        eo = jnp.einsum('enh,ehd->end', h, we2) + be2[:, None, :]
        y = xt + jnp.einsum('ne,end->nd', w, eo)
        return y.reshape(b, t, d)
    x = L0_attn_x
    xn = _layernorm(x, axis=-1)
    x = x + _L0_attn_ref(xn, L0_attn_in_proj_w, L0_attn_in_proj_b, L0_attn_conv_w, L0_attn_conv_b, L0_attn_bc_w, L0_attn_bc_b, L0_attn_dt_w, L0_attn_dt_b, L0_attn_A_log, L0_attn_D, L0_attn_out_w, L0_attn_out_b, L0_attn_ln_g, L0_attn_ln_b) + _L0_ffn_ref(xn, L0_ffn_rw1, L0_ffn_rb1, L0_ffn_rw2, L0_ffn_rb2, L0_ffn_we1, L0_ffn_be1, L0_ffn_we2, L0_ffn_be2)
    return x

_drawn_inputs = setup_inputs


def setup_inputs(seed=0):
    import zlib

    import numpy as np

    out = dict(_drawn_inputs(seed))
    spreads = {'L0_attn_in_proj_b': (0.0, 0.8),
     'L0_attn_conv_b': (0.0, 0.8),
     'L0_attn_bc_b': (0.0, 0.8),
     'L0_attn_dt_b': (0.0, 0.8),
     'L0_attn_D': (1.0, 0.6),
     'L0_attn_out_b': (0.0, 0.1),
     'L0_attn_ln_g': (1.0, 0.2),
     'L0_attn_ln_b': (0.0, 0.1),
     'L0_ffn_rb1': (0.0, 0.564),
     'L0_ffn_rb2': (0.0, 0.1),
     'L0_ffn_be1': (0.0, 0.8),
     'L0_ffn_be2': (0.0, 0.343)}
    factors = {'L0_attn_in_proj_w': 8.0,
     'L0_attn_conv_w': 8.0,
     'L0_attn_bc_w': 8.0,
     'L0_attn_dt_w': 8.0,
     'L0_attn_A_log': 8.0,
     'L0_attn_out_w': 8.0}
    for name, (base, spread) in spreads.items():
        noise = np.random.default_rng([zlib.crc32(name.encode()), seed]).standard_normal(out[name].shape)
        drawn = base * np.exp(spread * noise) if base else spread * noise
        out[name] = jnp.asarray(drawn.astype(out[name].dtype))
    for name, factor in factors.items():
        out[name] = (out[name] * factor).astype(out[name].dtype)
    return out
```

```python
from contextlib import ExitStack

import concourse.bass as bass
from concourse import mybir
from concourse.alu_op_type import AluOpType as ALU

ACT = mybir.ActivationFunctionType
AX = mybir.AxisListType
F32 = mybir.dt.float32
BF16 = mybir.dt.bfloat16
I32 = mybir.dt.int32

P = 128
B, L, D = 8, 512, 256
KD = D // P
NST, TAPS = 16, 4
E, H, TOPK = 8, 1024, 2
KH = H // P
TOK = B * L
TT = TOK // P
TB = L // P
EPS = 1e-5
MT = TOPK * TOK // P + E - 1
STEPS = 9
assert STEPS * B - 1 == MT
MC = MT + 3
PARTS = 96
BW = H + D

C_INB, C_CW, C_CB, C_DTB, C_D, C_AL, C_RB1, C_BCB, NCOL = 0, 4, 12, 14, 16, 18, 50, 52, 53
W_IN, W_BC, W_DT, W_OUT, NW = 0, 512, 608, 864, 1120
K_ID, K_IOTA, K_J, K_128, K_RST, K_TOK, K_PAD, NK = 0, 128, 256, 256 + MC, 288 + MC, 544 + MC, 576 + MC, 577 + MC


def held(eng, value):
    return value if isinstance(value, int) else eng.to_reg(value)


def build(nc, x, cols, rows, wmix, wroute, brows, we1, we2, consts, constb, out):
    ctx = ExitStack()
    with ctx:
        def sb(name, shape, dt=F32):
            return ctx.enter_context(nc.sbuf_tensor(name, shape, dt))

        def sem(name):
            return ctx.enter_context(nc.semaphore(name))

        psum = {n: ctx.enter_context(nc.psum_tensor("ps_" + n, [P, 512], F32))
                for n in ("up0", "up1", "tr0", "tr1", "yx", "bb", "bc", "fr")}

        xn_d = nc.dram_tensor("xn_scratch", [TOK, D], F32, kind="Internal").ap()
        xnt_d = nc.dram_tensor("xnt_scratch", [B * P, KD * L], F32, kind="Internal").ap()

        w1 = sb("w1", [P, E, KD, H])
        w2 = sb("w2", [P, E, KH, D])
        wm = sb("wm", [P, KD, NW])
        col = sb("col", [P, NCOL])
        dhalf = sb("dhalf", [P, KD])
        aneg = col[:, C_AL:C_AL + KD * NST].rearrange("p (k n) -> p k n", k=KD)
        gam = sb("gam", [P, D])
        ident = sb("ident", [P, P])
        sel = sb("sel", [PARTS, 32], BF16)
        bpart = sb("bpart", [PARTS, BW], BF16)
        bcpart = sb("bcpart", [PARTS, L], BF16)
        bcnext = sb("bcnext", [PARTS, L], BF16)
        te_i = sb("te_i", [P, MC], I32)
        gid = sb("gid", [P, MC], I32)
        sid = sb("sid", [P, MC], I32)
        wslot = sb("wslot", [P, MC])
        gcur = sb("gcur", [P, 1], I32)
        scur = sb("scur", [P, 1], I32)
        stat = sb("stat", [P, TB, 6])
        mv = sb("mv", [P, TB, 2])
        rstd = sb("rstd", [P, TB])
        ring = sb("ring", [P, 2, KD, L])
        da = sb("da", [P, 2, KD, L])
        xx = sb("xx", [P, 2, KD, L])
        xnt, xc = xx[:, 0, :, :], xx[:, 1, :, :]
        gs = sb("gs", [P, KD, L])
        dtt = sb("dtt", [P, KD, L])
        u = sb("u", [P, KD, L])
        xs = sb("xs", [P, KD, L + TAPS - 1])
        sp = sb("sp", [P, KD, L])
        y = sb("y", [P, KD, L])
        xtok = sb("xtok", [P, TB, D])
        xg = sb("xg", [P, D])
        xgt = sb("xgt", [P, KD, P])
        th = sb("th", [P, H])
        ht = sb("ht", [P, KH, P])
        yo = sb("yo", [P, D])

        rt_i = sb("rt_i", [P, TB], I32)
        scrap = sb("scrap", [P, 1])
        rt_t = sb("rt_t", [P, TB])
        RSQ = 12

        def rsqrt(dve, res, var, ti, tf, done, c):
            dve.tensor_scalar(var, var, EPS, None, ALU.add).then_inc(done, 1)
            dve.wait_ge(done, c + 1)
            dve.tensor_single_scalar(ti, var.bitcast(I32), 1, ALU.logical_shift_right).then_inc(done, 1)
            dve.wait_ge(done, c + 2)
            dve.tensor_scalar(res.bitcast(I32), ti, -1.0, float(0x5F3759DF), ALU.mult, ALU.add).then_inc(done, 1)
            for step in range(3):
                dve.wait_ge(done, c + 3 + 3 * step)
                dve.tensor_tensor(tf, res, res, ALU.mult).then_inc(done, 1)
                dve.wait_ge(done, c + 4 + 3 * step)
                dve.scalar_tensor_tensor(tf, tf, -0.5, var, ALU.mult, ALU.mult).then_inc(done, 1)
                dve.wait_ge(done, c + 5 + 3 * step)
                dve.scalar_tensor_tensor(res, tf, 1.5, res, ALU.add, ALU.mult).then_inc(done, 1)
            dve.wait_ge(done, c + RSQ)

        s_const = sem("s_const")
        s_w = sem("s_w")

        def flat(a):
            return a.rearrange("p k l -> p (k l)")

        xall = w2.rearrange("p e k d -> p (e k) d")[:, 0:TT, :]
        xnb = [da[:, q, :, :].rearrange("p k (j f) -> p (k j) f", j=2) for q in range(2)]
        head = flat(u[:, :, :])
        stat1 = head[:, 0:6 * TT].rearrange("p (t s) -> p t s", s=6)
        mv1 = head[:, 6 * TT:8 * TT].rearrange("p (t s) -> p t s", s=2)
        rstd1, tf1 = head[:, 8 * TT:9 * TT], head[:, 9 * TT:10 * TT]
        ti1 = head[:, 10 * TT:11 * TT].bitcast(I32)
        rowb = flat(u[:, :, :])[:, 384:384 + D + E]
        ks = flat(sp[:, :, :])[:, 0:NK - P]
        tri = flat(sp[:, :, :])[:, NK - P:NK - P + P // 2].bitcast(BF16)
        ones = flat(sp[:, :, :])[:, NK - P // 2:NK].bitcast(BF16)
        spare = w2.rearrange("p e k d -> p (e k d)")[0:PARTS, TT * D:TT * D + BW]
        stage0, stage1 = spare[:, 0:H], spare[:, H:BW]
        xtb = [xnt, xc]
        rv = [gs, dtt]
        rt = y
        wr = th[:, 0:KD * 264].rearrange("p (k n) -> p k n", k=KD)
        logit = xtok[:, 0, :].rearrange("p (t e) -> p t e", e=E)
        x_v = x.rearrange("(b j p) d -> b p j d", p=P, j=TB)
        xn_v = xn_d.rearrange("(b j p) d -> b p j d", p=P, j=TB)
        out_v = out.rearrange("(b j p) d -> b p j d", p=P, j=TB)
        we1_v = we1.rearrange("e (k p) h -> e p k h", p=P)
        xnt_v = xnt_d.rearrange("(b p) (k l) -> b p k l", p=P, k=KD)

        s_l2 = sem("s_l2")
        nslot_big = xtok[:, :, :].rearrange("p j f -> p (j f)")[:, 0:E * MC]
        XP = 4
        s_x = [sem(f"s_x{q}") for q in range(XP)]
        s_st = sem("s_st")
        s_ag = sem("s_ag")
        s_rs = sem("s_rs")
        s_xn = sem("s_xn")
        s_res = sem("s_res")
        s_xnw = [sem(f"s_xnw{q}") for q in range(2)]
        s_acc = sem("s_acc")
        s_xtw = [sem(f"s_xtw{q}") for q in range(2)]
        s_k2 = sem("s_k2")
        s_brow = sem("s_brow")
        s_pb = sem("s_pb")
        s_brd = sem("s_brd")
        s_tr = sem("s_tr")
        s_xt = sem("s_xt")
        s_rm = sem("s_rm")
        s_rv = sem("s_rv")
        s_rt = sem("s_rt")
        s_rs2 = sem("s_rs2")
        s_lg = sem("s_lg")
        s_lg2 = sem("s_lg2")
        s_const2 = sem("s_const2")
        s_scaled = sem("s_scaled")

        with nc.Block() as block:
            @block.sync
            def _(sync):
                for piece in range(XP):
                    n = TT // XP
                    sync.dma_start(xall[:, piece * n:(piece + 1) * n, :],
                                   x.rearrange("(t p) d -> p t d", p=P)[:, piece * n:(piece + 1) * n, :]
                                   ).then_inc(s_x[piece], 16)

                def store(h, q):
                    sync.wait_ge(s_xn, h * 8 + 4 * q + 4)
                    sync.dma_start(xn_v[h * 2 + q], xnb[q]).then_inc(s_xnw[q], 16)
                    sync.wait_ge(s_xt, h * 4 + 2 * q + 2)
                    sync.dma_start(xnt_v[h * 2 + q], xtb[q]).then_inc(s_xtw[q], 16)
                    sync.dma_start(w1[:, bass.ds(h * 2 + q, 1), :, :], we1_v[h * 2 + q]).then_inc(s_w, 16)

                with sync.Fori(0, B // 2) as i:
                    for q in range(2):
                        store(i, q)
                for q in range(2):
                    sync.wait_ge(s_xnw[q], 16 * B // 2)
                    sync.wait_ge(s_xtw[q], 16 * B // 2)

            @block.gpsimd
            def _(pool):
                for r in range(3):
                    pool.dma_start(spare[32 * r:32 * r + 32, :], brows).then_inc(s_brow, 16)
                pool.wait_ge(s_brow, 48)
                n = [0]

                def link(ins):
                    n[0] += 1
                    ins.then_inc(s_pb, 1)
                    pool.wait_ge(s_pb, n[0])

                for part, (st_, lo, hi) in enumerate(((stage0, 0, H), (stage1, H, BW))):
                    bp = bpart[:, lo:hi]
                    link(pool.tensor_copy(bp, st_))
                    link(pool.tensor_tensor(st_, st_, bp, ALU.subtract))
                    link(pool.tensor_copy(bp[32:64, :], st_[32:64, :]))
                    link(pool.tensor_copy(bp[64:96, :], st_[64:96, :]))
                    pool.tensor_tensor(bp[64:96, :], st_[64:96, :], bp[64:96, :], ALU.subtract).then_inc(s_brd, 1)
                    pool.wait_ge(s_brd, part + 1)

                with pool.Fori(0, B // 2) as i:
                    for q in range(2):
                        n = i * 2 + q
                        xa = xall[:, bass.ts(n, TB), :]
                        normed, summed = held(pool, n * 4 + 4), held(pool, n * 2 + 1)
                        pool.wait_ge(s_const2, 48)
                        pool.wait_ge(s_xn, normed)
                        pool.tensor_tensor(xa, xa, xnb[q], ALU.add).then_inc(s_res, 1)
                        pool.wait_ge(s_const2, 48)
                        pool.wait_ge(s_res, summed)
                        pool.tensor_tensor(xa, xa, rowb[:, 0:D].unsqueeze(1).to_broadcast([P, TB, D]),
                                           ALU.add).then_inc(s_res, 1)
                        pool.wait_ge(s_res, n * 2 + 2)
                        pool.dma_start(out_v[n], xa).then_inc(s_acc, 16)
                pool.wait_ge(s_acc, 16 * B)

            @block.vector
            def _(dve):
                def tokens(first, last, c):
                    n = TT // XP
                    for piece in range(first, last):
                        dve.wait_ge(s_x[piece], 16)
                        for t in range(piece * n, piece * n + n):
                            dve.bn_stats(stat1[:, t, :], xall[:, t, :]).then_inc(s_st, 1)
                        dve.wait_ge(s_st, piece * n + n)
                        for t in range(piece * n, piece * n + n):
                            dve.bn_aggr(mv1[:, t, :], stat1[:, t, :]).then_inc(s_ag, 1)
                    dve.wait_ge(s_ag, last * n)
                    at = slice(first * n, last * n)
                    rsqrt(dve, rstd1[:, at], mv1[:, at, 1], ti1[:, at], tf1[:, at], s_rs, c)

                def norm(h, q):
                    if not isinstance(h, int):
                        dve.wait_ge(s_xnw[q], h * 16)
                        dve.wait_ge(s_tr, (h * 2 + q) * 2 - 2)
                        dve.wait_ge(s_res, (h * 2 + q) * 2 - 2)
                    for j in range(TB):
                        t = (h * 2 + q) * TB + j
                        dve.tensor_scalar(xnb[q][:, j, :], xall[:, bass.ds(t, 1), :], mv1[:, bass.ds(t, 1), 0],
                                          rstd1[:, bass.ds(t, 1)], ALU.subtract, ALU.mult).then_inc(s_xn, 1)

                def hidden(h, q):
                    for m in range(KD):
                        dve.wait_ge(s_rt, h * 4 + 2 * q + m + 1)
                        dve.scalar_tensor_tensor(rv[q][:, m, :], rt[:, m, :], 1.0, rv[q][:, m, :],
                                                 ALU.add, ALU.mult).then_inc(s_rs2, 1)

                tokens(0, 1, 0)
                norm(0, 0)
                norm(0, 1)
                tokens(1, XP, RSQ)
                dve.wait_ge(s_const, 64)
                dve.tensor_scalar(wr[:, :, 256:264], wr[:, :, 256:264], 0.5, None, ALU.mult).then_inc(s_scaled, 1)
                dve.tensor_scalar(dhalf[:, :], col[:, C_D:C_D + KD], 0.5, None, ALU.mult).then_inc(s_scaled, 1)
                dve.tensor_scalar(wm[:, :, W_BC:W_OUT], wm[:, :, W_BC:W_OUT], 0.5, None, ALU.mult).then_inc(s_scaled, 1)
                with dve.Fori(0, B // 2 - 1) as i:
                    norm(i + 1, 0)
                    hidden(i, 0)
                    norm(i + 1, 1)
                    hidden(i, 1)
                hidden(B // 2 - 1, 0)
                hidden(B // 2 - 1, 1)

            @block.tensor
            def _(pe):
                def turn(h, q):
                    pe.wait_ge(s_xn, h * 8 + 4 * q + 4)
                    pe.wait_ge(s_xt, h * 4 + 2 * q)
                    for k in range(KD):
                        ps = psum[f"up{k}"]
                        for j in range(TB):
                            mm = pe.transpose(ps[:, j * P:(j + 1) * P], xnb[q][:, j, k * P:(k + 1) * P], ident[:, :])
                        mm.then_inc(s_tr, 1)

                def route(h, q):
                    pe.wait_ge(s_xt, h * 4 + 2 * q + 2)
                    pe.wait_ge(s_rv, h * 4 + 2 * q)
                    for m in range(KD):
                        for k in range(KD):
                            mm = pe.matmul(psum[f"tr{m}"][:, :], wr[:, k, m * P:(m + 1) * P], xtb[q][:, k, :],
                                           start=(k == 0), stop=(k == KD - 1))
                        mm.then_inc(s_rm, 1)

                def logits(h, q):
                    pe.wait_ge(s_rs2, h * 4 + 2 * q + 2)
                    pe.wait_ge(s_lg, h * 2 + q)
                    for j in range(TB):
                        for k in range(KD):
                            mm = pe.matmul(psum["yx"][:, j * E:(j + 1) * E], rv[q][:, k, j * P:(j + 1) * P],
                                           wr[:, k, 256:264], start=(k == 0), stop=(k == KD - 1))
                    mm.then_inc(s_lg2, 1)

                pe.wait_ge(s_const, 64)
                turn(0, 0)
                turn(0, 1)
                route(0, 0)
                pe.wait_ge(s_scaled, 3)
                with pe.Fori(0, B // 2 - 1) as i:
                    turn(i + 1, 0)
                    route(i, 1)
                    logits(i, 0)
                    turn(i + 1, 1)
                    route(i + 1, 0)
                    logits(i, 1)
                route(B // 2 - 1, 1)
                logits(B // 2 - 1, 0)
                logits(B // 2 - 1, 1)

            @block.scalar
            def _(act):
                act.dma_start(col[:, :], cols).then_inc(s_const, 16)
                act.dma_start(ident[:, :], consts[:, K_ID:K_ID + P]).then_inc(s_const, 16)
                act.dma_start(wr, wroute).then_inc(s_const, 16)
                act.dma_start(wm[:, :, :], wmix).then_inc(s_const, 16)
                act.dma_start(gam[:, :], rows[0:D].partition_broadcast(P)).then_inc(s_const2, 16)
                act.dma_start(rowb, rows[D:2 * D + E].partition_broadcast(P)).then_inc(s_const2, 16)
                act.dma_start(sel[:, :], constb[0:PARTS, 2 * P:2 * P + 32]).then_inc(s_const2, 16)
                act.dma_start(ks, consts[:, P:NK]).then_inc(s_k2, 16)
                act.dma_start(flat(sp[:, :, :])[:, NK - P:NK].bitcast(BF16), constb[:, 0:2 * P]).then_inc(s_k2, 16)

                def copy_xt(h, q):
                    act.wait_ge(s_xtw[q], h * 16)
                    for k in range(KD):
                        act.wait_ge(s_tr, h * 4 + 2 * q + k + 1)
                        act.activation(xtb[q][:, k, :], psum[f"up{k}"][:, :], ACT.Copy).then_inc(s_xt, 1)

                def hidden(h, q):
                    act.wait_ge(s_rs2, h * 4 + 2 * q)
                    for m in range(KD):
                        act.wait_ge(s_rm, h * 4 + 2 * q + m + 1)
                        act.activation(rv[q][:, m, :], psum[f"tr{m}"][:, :], ACT.Identity,
                                       bias=col[:, C_RB1 + m:C_RB1 + m + 1]).then_inc(s_rv, 1)
                        act.wait_ge(s_rv, h * 4 + 2 * q + m + 1)
                        act.activation(rt[:, m, :], rv[q][:, m, :], ACT.Tanh, scale=0.5).then_inc(s_rt, 1)

                def copy_logits(h, q):
                    act.wait_ge(s_lg2, h * 2 + q + 1)
                    act.activation(logit[:, bass.ts(h * 2 + q, TB), :],
                                   psum["yx"][:, 0:TB * E].rearrange("p (j e) -> p j e", e=E),
                                   ACT.Copy).then_inc(s_lg, 1)

                act.wait_ge(s_const, 64)
                copy_xt(0, 0)
                copy_xt(0, 1)
                hidden(0, 0)
                with act.Fori(0, B // 2 - 1) as i:
                    copy_xt(i + 1, 0)
                    hidden(i, 1)
                    copy_logits(i, 0)
                    copy_xt(i + 1, 1)
                    hidden(i + 1, 0)
                    copy_logits(i, 1)
                hidden(B // 2 - 1, 1)
                copy_logits(B // 2 - 1, 0)
                copy_logits(B // 2 - 1, 1)

        smalls = [flat(dtt[:, :, :])[:, i * 256:(i + 1) * 256] for i in range(4)] + \
                 [xtok[:, i, :] for i in range(1, 4)] + [flat(ht[:, :, :])[:, i * 256:(i + 1) * 256] for i in range(4)]
        et = [a.rearrange("p (e t) -> p e t", e=E) for a in smalls]
        lg, rank, beats, top0, top1, incl, slot, tmp, nslot = et[:9]
        k_iota, k_j = ks[:, K_IOTA - P:K_J - P], ks[:, K_J - P:K_128 - P]
        k_128, k_rst = ks[:, K_128 - P:K_RST - P], ks[:, K_RST - P:K_TOK - P]
        k_tok, k_pad = ks[:, K_TOK - P:K_PAD - P], ks[:, K_PAD - P:NK - P]
        both = th[:, P:2 * P].bitcast(BF16)
        KT = TOPK * TT
        pv = th[:, 256:1024].rearrange("p (n c) -> p n c", c=KT)
        slotf, af, bf, idv, wv, l01, e2 = (pv[:, i, :] for i in range(7))
        sloti, ai, bi = (pv[:, i, :].bitcast(I32) for i in range(7, 10))
        em = pv[:, 10, :]
        cnt, nt, sinc, st = em[:, 0:8], em[:, 8:16], em[:, 16:24], em[:, 24:32]
        st128, unit = em[:, 32:40], em[:, 40:48]
        CH = 8
        NCH = KT // CH
        ob = [ring[:, q, :, :].rearrange("p k (a c) -> p (k a) c", c=P) for q in range(2)]
        oa = [flat(y[:, :, :])[:, 0:CH * MC].rearrange("p (a c) -> p a c", c=MC),
              flat(u[:, :, :])[:, 0:CH * MC].rearrange("p (a c) -> p a c", c=MC)]
        ov = [a.rearrange("p b k l -> p (b k l)")[:, 0:CH * 2 * MC].rearrange("p (a v c) -> p a v c", v=2, c=MC)
              for a in (da[:, :, :, :], xx[:, :, :, :])]

        s_dch = sem("s_dch")
        s_l = sem("s_l")
        s_e2 = sem("s_e2")
        s_both = sem("s_both")
        s_cum = sem("s_cum")
        s_val = sem("s_val")
        s_ob = sem("s_ob")
        s_obh = sem("s_obh")
        s_oa = sem("s_oa")
        s_ov = sem("s_ov")
        s_idm = sem("s_idm")
        s_tab = sem("s_tab")

        with nc.Block() as block:
            @block.sync
            def _(sync):
                for e in range(E):
                    sync.dma_start(w2[:, e, :, :], we2[e].rearrange("(k p) d -> p k d", p=P)).then_inc(s_w, 16)

            @block.scalar
            def _(act):
                act.wait_ge(s_l, 1)
                act.activation(e2[:, 0:TT], l01[:, 0:TT], ACT.Exp).then_inc(s_e2, 1)

            @block.gpsimd
            def _(pool):
                def weights_in(i, q, first=False):
                    placed, rows_in = held(pool, i * 2 + q - 1), held(pool, i * 2 + q + 1)
                    pool.wait_ge(s_val, 1)
                    if not first:
                        pool.wait_ge(s_idm, placed)
                    pool.wait_ge(s_oa, rows_in)
                    pool.tensor_tensor(ov[q][:, :, 1, :], oa[q],
                                       wv[:, bass.ts(i * 2 + q, CH)].unsqueeze(2).to_broadcast([P, CH, MC]),
                                       ALU.mult).then_inc(s_ov, 1)

                weights_in(0, 0, True)
                weights_in(0, 1, True)
                with pool.Fori(1, NCH // 2) as i:
                    weights_in(i, 0)
                    weights_in(i, 1)

            @block.tensor
            def _(pe):
                pe.wait_ge(s_both, 1)
                pe.matmul(psum["bb"][:, 0:256], tri, both, start=True, stop=True).then_inc(s_cum, 1)
                pe.matmul(psum["bc"][:, 0:256], ones, both, start=True, stop=True).then_inc(s_cum, 1)

                def place(i, q, a, first, last):
                    return pe.matmul(psum["fr"][:, 0:2 * MC], ob[q][:, a, :],
                                     ov[q][:, a, :, :].rearrange("p v c -> p (v c)"), start=first, stop=last)

                def chunk(i, q, first, last):
                    pe.wait_ge(s_ob, i * 2 + q + 1)
                    pe.wait_ge(s_ov, i * 2 + q + 1)
                    for a in range(CH):
                        mm = place(i, q, a, first and a == 0, last and a == CH - 1)
                    mm.then_inc(s_idm, 1)

                chunk(0, 0, True, False)
                chunk(0, 1, False, False)
                with pe.Fori(1, NCH // 2 - 1) as i:
                    chunk(i, 0, False, False)
                    chunk(i, 1, False, False)
                chunk(NCH // 2 - 1, 0, False, False)
                chunk(NCH // 2 - 1, 1, False, True)

            @block.vector
            def _(dve):
                steps = [0]

                def link(ins):
                    steps[0] += 1
                    ins.then_inc(s_dch, 1)
                    dve.wait_ge(s_dch, steps[0])

                dve.wait_ge(s_k2, 32)
                dve.wait_ge(s_const2, 48)
                link(dve.tensor_tensor(lg, logit.rearrange("p t e -> p e t"),
                                       rowb[:, D:D + E].unsqueeze(2).to_broadcast([P, E, TT]), ALU.add))
                link(dve.memset(rank, 0.0))
                for j in range(E):
                    one = lg[:, j:j + 1, :]
                    if j > 0:
                        dve.tensor_tensor(beats[:, 0:j, :], one.to_broadcast([P, j, TT]), lg[:, 0:j, :], ALU.is_gt).then_inc(s_l2, 1)
                    if j < E - 1:
                        dve.tensor_tensor(beats[:, j + 1:E, :], one.to_broadcast([P, E - 1 - j, TT]),
                                          lg[:, j + 1:E, :], ALU.is_ge).then_inc(s_l2, 1)
                    if 0 < j < E - 1:
                        dve.wait_ge(s_l2, 2 * j + 1)
                        link(dve.memset(beats[:, j, :], 0.0))
                        link(dve.tensor_tensor(rank, rank, beats, ALU.add))
                    elif j == 0:
                        dve.wait_ge(s_l2, 1)
                        link(dve.tensor_tensor(rank[:, 1:E, :], rank[:, 1:E, :], beats[:, 1:E, :], ALU.add))
                    else:
                        dve.wait_ge(s_l2, 2 * j)
                        link(dve.tensor_tensor(rank[:, 0:j, :], rank[:, 0:j, :], beats[:, 0:j, :], ALU.add))
                dve.tensor_scalar(both.rearrange("p (e t) -> p e t", e=E), rank, float(TOPK), None,
                                  ALU.is_lt).then_inc(s_both, 1)
                for k, top in enumerate((top0, top1)):
                    link(dve.tensor_scalar(top, rank, float(k), None, ALU.is_equal))
                    link(dve.tensor_tensor(tmp, top, lg, ALU.mult))
                    link(dve.tensor_reduce(af[:, k * TT:(k + 1) * TT], tmp.rearrange("p e t -> p t e"), AX.X, ALU.add))
                dve.tensor_tensor(l01[:, 0:TT], af[:, TT:2 * TT], af[:, 0:TT], ALU.subtract).then_inc(s_l, 1)
                dve.wait_ge(s_cum, 2)
                tot = psum["bc"][:, 0:256]
                link(dve.tensor_tensor_scan(incl.rearrange("p e t -> p (e t)"), k_rst, tot, 0.0, ALU.mult, ALU.add))
                link(dve.tensor_tensor(slot, incl, tot.rearrange("p (e t) -> p e t", e=E), ALU.subtract))
                link(dve.tensor_copy(cnt, incl[:, :, TT - 1]))
                link(dve.tensor_tensor(tmp, cnt.unsqueeze(2).to_broadcast([P, E, TT]),
                                       k_128.unsqueeze(1).to_broadcast([P, E, TT]), ALU.is_gt))
                link(dve.tensor_reduce(nt, tmp, AX.X, ALU.add))
                link(dve.memset(unit, 1.0))
                link(dve.tensor_tensor_scan(sinc, unit, nt, 0.0, ALU.mult, ALU.add))
                link(dve.tensor_tensor(st, sinc, nt, ALU.subtract))
                link(dve.tensor_scalar(st128, st, float(P), None, ALU.mult))
                link(dve.tensor_tensor(slot, slot, psum["bb"][:, 0:256].rearrange("p (e t) -> p e t", e=E), ALU.add))
                link(dve.tensor_tensor(slot, slot, st128.unsqueeze(2).to_broadcast([P, E, TT]), ALU.add))
                for k, top in enumerate((top0, top1)):
                    link(dve.tensor_tensor(tmp, top, slot, ALU.mult))
                    link(dve.tensor_reduce(slotf[:, k * TT:(k + 1) * TT], tmp.rearrange("p e t -> p t e"), AX.X, ALU.add))
                link(dve.tensor_copy(sloti, slotf))
                link(dve.tensor_single_scalar(ai, sloti, 7, ALU.logical_shift_right))
                link(dve.tensor_single_scalar(bi, sloti, P - 1, ALU.bitwise_and))
                link(dve.tensor_copy(af, ai))
                link(dve.tensor_copy(bf, bi))
                link(dve.tensor_tensor(idv.rearrange("p (k t) -> p k t", k=TOPK),
                                       k_tok.unsqueeze(1).to_broadcast([P, TOPK, TT]),
                                       bf.rearrange("p (k t) -> p k t", k=TOPK), ALU.subtract))
                dve.wait_ge(s_e2, 1)
                link(dve.tensor_scalar(l01[:, TT:2 * TT], e2[:, 0:TT], 1.0, None, ALU.add))
                link(dve.reciprocal(wv[:, 0:TT], l01[:, TT:2 * TT]))
                dve.tensor_tensor(wv[:, TT:2 * TT], e2[:, 0:TT], wv[:, 0:TT], ALU.mult).then_inc(s_val, 1)

                def one_hot(i, q, first=False):
                    if not first:
                        dve.wait_ge(s_ov, i * 2 + q - 1)
                    dve.tensor_tensor(oa[q], k_j.unsqueeze(1).to_broadcast([P, CH, MC]),
                                      af[:, bass.ts(i * 2 + q, CH)].unsqueeze(2).to_broadcast([P, CH, MC]),
                                      ALU.is_equal).then_inc(s_oa, 1)
                    if not first:
                        dve.wait_ge(s_idm, i * 2 + q - 1)
                    dve.tensor_tensor(ob[q], k_iota.unsqueeze(1).to_broadcast([P, CH, P]),
                                      bf[:, bass.ts(i * 2 + q, CH)].unsqueeze(2).to_broadcast([P, CH, P]),
                                      ALU.is_equal).then_inc(s_obh, 1)
                    dve.wait_ge(s_oa, i * 2 + q + 1)
                    dve.tensor_tensor(ov[q][:, :, 0, :], oa[q],
                                      idv[:, bass.ts(i * 2 + q, CH)].unsqueeze(2).to_broadcast([P, CH, MC]),
                                      ALU.mult).then_inc(s_ob, 1)

                one_hot(0, 0, True)
                one_hot(0, 1, True)
                with dve.Fori(1, NCH // 2) as i:
                    one_hot(i, 0)
                    one_hot(i, 1)
                big = nslot_big.rearrange("p (c e) -> p c e", e=E)
                link(dve.tensor_tensor(big, st.unsqueeze(1).to_broadcast([P, MC, E]),
                                       k_j.unsqueeze(2).to_broadcast([P, MC, E]), ALU.is_le))
                link(dve.tensor_reduce(wslot[:, :], big, AX.X, ALU.add))
                link(dve.tensor_scalar(te_i[:, :], wslot[:, :], -1.0, None, ALU.add))
                dve.wait_ge(s_idm, NCH)
                ids = psum["fr"][:, 0:MC]
                link(dve.tensor_scalar(sid[:, :], ids, k_pad, None, ALU.add))
                dve.tensor_copy(wslot[:, :], psum["fr"][:, MC:2 * MC]).then_inc(s_tab, 1)
                dve.tensor_scalar(gid[:, :], ids, k_pad, float(TOK - 1), ALU.add, ALU.min).then_inc(s_tab, 1)

        s_sum = sem("s_sum")
        s_dafree = sem("s_dafree")
        s_an = sem("s_an")
        s_an0 = sem("s_an0")
        s_xnt = sem("s_xnt")
        s_xtok = sem("s_xtok")
        s_frdy = sem("s_frdy")
        s_ffree = sem("s_ffree")
        s_gt = sem("s_gt")
        s_gs = sem("s_gs")
        s_tap = sem("s_tap")
        s_ct = sem("s_ct")
        s_xv = sem("s_xv")
        s_part = sem("s_part")
        s_bcp = sem("s_bcp")
        s_sp = sem("s_sp")
        s_v = sem("s_v")
        s_dtt = sem("s_dtt")
        s_u = sem("s_u")
        s_y0 = sem("s_y0")
        s_yg = sem("s_yg")
        s_o1 = sem("s_o1")
        s_z1 = sem("s_z1")
        s_bb = sem("s_bb")
        s_bcr = sem("s_bcr")
        s_um = sem("s_um")
        s_da = sem("s_da")
        s_hc = sem("s_hc")
        s_zs = sem("s_zs")
        s_za = sem("s_za")
        s_zr = sem("s_zr")
        s_zn = sem("s_zn")
        s_zg = sem("s_zg")
        s_gc = sem("s_gc")
        s_sc = sem("s_sc")
        s_xg = sem("s_xg")
        s_xtr = sem("s_xtr")
        s_xtc = sem("s_xtc")
        s_up = sem("s_up")
        s_th = sem("s_th")
        s_hs = sem("s_hs")
        s_t = sem("s_t")
        s_ht = sem("s_ht")
        s_dn = sem("s_dn")
        s_y = sem("s_y")
        s_sct = sem("s_sct")

        IN = 8
        NU = NST // IN
        xsv = xs[:, :, TAPS - 1:]
        bcf = sp[0:PARTS, 1, :]
        yx_y, tr_x = psum["yx"][:, 0:D], psum["tr1"][:, 0:D]
        F_G0, F_G1, F_IN0, F_IN1, F_BC, F_DT0, F_DT1, F_OUT = range(5, 13)
        FS = 8
        F_OUT_LAST = F_OUT - 5

        def positive(n):
            return not isinstance(n, int) or n > 0

        with nc.Block() as block:
            @block.sync
            def _(sync):
                sync.dma_start(xnt, xnt_v[0]).then_inc(s_xnt, 16)
                sync.dma_start(xtok[:, :, :], xn_v[0]).then_inc(s_xtok, 16)

                def load_xnt(b):
                    sync.wait_ge(s_frdy, b * FS - FS + F_G1 + 1)
                    sync.dma_start(xnt, xnt_v[b]).then_inc(s_xnt, 16)

                def load_xtok(b):
                    sync.wait_ge(s_acc, (b + B) * 16)
                    sync.dma_start(xtok[:, :, :], xn_v[b]).then_inc(s_xtok, 16)

                load_xnt(1)
                with sync.Fori(0, B - 2) as b:
                    load_xnt(b + 2)
                    load_xtok(b + 1)
                load_xtok(B - 1)

            @block.gpsimd
            def _(pool):
                def gather(j):
                    if positive(j):
                        pool.wait_ge(s_xg, j * 16)
                    pool.tensor_copy(gcur[:, :], gid[:, bass.ds(j, 1)]).then_inc(s_gc, 1)
                    this, last = held(pool, j + 1), held(pool, j)
                    pool.wait_ge(s_tab, 2)
                    pool.wait_ge(s_gc, this)
                    if positive(j):
                        pool.wait_ge(s_xtr, last)
                    pool.indirect_dma_start(xg[:, :], None, xn_d[:, :],
                                            bass.IndirectOffsetOnAxis(ap=gcur[:, :], axis=0)).then_inc(s_xg, 16)

                def scatter(s, b, i):
                    if positive(s):
                        pool.wait_ge(s_sct, s * 16)
                    if i == 4:
                        pool.wait_ge(s_acc, (b + B) * 16)
                    pool.tensor_copy(scur[:, :], sid[:, bass.ds(s, 1)]).then_inc(s_sc, 1)
                    this = held(pool, s + 1)
                    pool.wait_ge(s_tab, 2)
                    pool.wait_ge(s_sc, this)
                    pool.wait_ge(s_y, this)
                    pool.indirect_dma_start(out[:, :], bass.IndirectOffsetOnAxis(ap=scur[:, :], axis=0), yo[:, :], None,
                                            bounds_check=TOK - 1, oob_is_err=False,
                                            compute_op=ALU.add).then_inc(s_sct, 16)

                def add_state(b, i, r):
                    g = b * NST + i * NU + r
                    if i == 0 and r == 0:
                        pool.wait_ge(s_y0, (b + 1) * KD)
                    if positive(g):
                        pool.wait_ge(s_sum, g)
                    pool.wait_ge(s_hc, g + 1)
                    pool.tensor_tensor(y[:, :, :], y[:, :, :], ring[:, r, :, :], ALU.add).then_inc(s_sum, 1)

                def finish(b, tiles):
                    pool.wait_ge(s_zn, (b + 1) * TB)
                    pool.tensor_tensor(xtok[:, :, :], xtok[:, :, :],
                                       gam[:, :].unsqueeze(1).to_broadcast([P, TB, D]), ALU.mult).then_inc(s_zg, 1)
                    pool.wait_ge(s_sct, tiles * 16)
                    pool.wait_ge(s_zg, b + 1)
                    pool.dma_start(out_v[b], xtok[:, :, :], accum_op=ALU.add).then_inc(s_acc, 16)

                def step(b, i, prev=None, last=False):
                    s = b * STEPS + i
                    if i < IN:
                        add_state(b, i, 0)
                    if not (last and i >= STEPS - 4):
                        gather(s + 3)
                    if not (last and i == STEPS - 1):
                        scatter(s, b, i)
                    if i < IN:
                        add_state(b, i, 1)
                    if i == 3 and prev is not None:
                        finish(prev, s + 1)

                pool.wait_ge(s_acc, 16 * B)
                for j in range(3):
                    gather(j)
                for i in range(4):
                    step(0, i)
                with pool.Fori(0, B - 1) as b:
                    for i in range(4, STEPS):
                        step(b, i)
                    for i in range(4):
                        step(b + 1, i, prev=b)
                for i in range(4, STEPS):
                    step(B - 1, i, last=True)
                finish(B - 1, MT)
                pool.wait_ge(s_xg, 16 * MT)
                pool.wait_ge(s_sct, 16 * MT)
                pool.wait_ge(s_acc, 16 * 2 * B)

            @block.scalar
            def _(act):
                act.activation(aneg, aneg, ACT.Exp).then_inc(s_an, 1)

                def conv_in(b, m, f):
                    act.wait_ge(s_frdy, f + 1)
                    if positive(b):
                        act.wait_ge(s_dtt, b)
                    act.activation(xsv[:, m, :], psum["fr"][:, :], ACT.Identity,
                                   bias=col[:, C_INB + m:C_INB + m + 1]).then_inc(s_ffree, 1)

                def gate_in(b, m, f):
                    if positive(b) and m == 0:
                        act.wait_ge(s_yg, b)
                    act.wait_ge(s_frdy, f + 1)
                    act.activation(gs[:, m, :], psum["fr"][:, :], ACT.Identity,
                                   bias=col[:, C_INB + KD + m:C_INB + KD + m + 1]).then_inc(s_ffree, 1)
                    act.wait_ge(s_dtt, b + 1)
                    act.wait_ge(s_ffree, f + 1)
                    act.activation(sp[:, m, :], gs[:, m, :], ACT.Tanh, scale=0.5).then_inc(s_gt, 1)

                def conv_tanh(b):
                    for m in range(KD):
                        act.wait_ge(s_tap, b * 8 + 8)
                        act.activation(xsv[:, m, :], xc[:, m, :], ACT.Tanh, scale=0.5).then_inc(s_ct, 1)

                def bc_in(b, f):
                    if positive(b):
                        act.wait_ge(s_gs, b * KD)
                    act.wait_ge(s_frdy, f + 1)
                    act.activation(bcf, psum["fr"][0:PARTS, :], ACT.Identity,
                                   bias=col[0:PARTS, C_BCB:C_BCB + 1]).then_inc(s_ffree, 1)

                def dt_in(b, m, f):
                    act.wait_ge(s_frdy, f + 1)
                    if m == 1:
                        act.wait_ge(s_part, b * 5 + 5)
                    act.activation(sp[:, m, :], psum["fr"][:, :], ACT.Abs,
                                   bias=col[:, C_DTB + m:C_DTB + m + 1]).then_inc(s_sp, 1)
                    act.activation(xsv[:, m, :], psum["fr"][:, :], ACT.Identity,
                                   bias=col[:, C_DTB + m:C_DTB + m + 1]).then_inc(s_ffree, 1)

                def exp_dt(b):
                    act.wait_ge(s_sp, b * 4 + 2)
                    act.activation(sp[:, :, :], sp[:, :, :], ACT.Exp, scale=-1.0).then_inc(s_sp, 1)

                def ln_dt(b):
                    act.wait_ge(s_sp, b * 4 + 3)
                    act.activation(sp[:, :, :], sp[:, :, :], ACT.Ln, bias=1.0).then_inc(s_sp, 1)
                    act.activation(scrap[:, :], col[:, 0:1], ACT.Exp)

                def decay(b, i, r):
                    g = b * NST + i * NU + r
                    if i == 0 and r == 0:
                        act.wait_ge(s_dtt, b + 1)
                    act.wait_ge(s_dafree, g + 1)
                    for k in range(KD):
                        n = i * NU + r
                        act.activation(da[:, r, k, 1:], dtt[:, k, 1:], ACT.Exp,
                                       scale=aneg[:, k, n:n + 1]).then_inc(s_da, 1)

                def copy_x(j):
                    act.wait_ge(s_xtr, j + 1)
                    if positive(j):
                        act.wait_ge(s_up, j * 2)
                    act.activation(xgt[:, :, :], tr_x.rearrange("p (k c) -> p k c", k=KD), ACT.Copy).then_inc(s_xtc, 1)

                def tanh_h(j, h):
                    act.wait_ge(s_up, j * 2 + h + 1)
                    if h == 0 and positive(j):
                        act.wait_ge(s_t, j * 2)
                    act.activation(th[:, h * 512:(h + 1) * 512], psum[f"up{h}"][:, :], ACT.Tanh,
                                   scale=0.5).then_inc(s_th, 1)

                def copy_h(j):
                    for h in range(2):
                        act.wait_ge(s_t, j * 2 + h + 1)
                        if h == 0 and positive(j):
                            act.wait_ge(s_dn, j)
                        act.activation(ht[:, 4 * h:4 * h + 4, :],
                                       psum[f"tr{h}"][:, :].rearrange("p (k c) -> p k c", c=P), ACT.Copy,
                                       scale=0.5).then_inc(s_ht, 1)

                def weigh(j):
                    act.wait_ge(s_dn, j + 1)
                    if positive(j):
                        act.wait_ge(s_sct, j * 16)
                    act.activation(yo[:, :], yx_y, ACT.Copy, scale=wslot[:, bass.ds(j, 1)]).then_inc(s_y, 1)

                def step(b, i, last=False):
                    s, f = b * STEPS + i, b * FS
                    prepare = not last
                    if i < IN:
                        decay(b, i, 0)
                    if not (last and i == STEPS - 1):
                        copy_h(s)
                    if i == 8 and prepare:
                        ln_dt(b + 1)
                    if not (last and i >= STEPS - 2):
                        for h in range(2):
                            tanh_h(s + 1, h)
                    if i in (0, 1):
                        gate_in(b, i, f + F_G0 + i)
                    if i == 6 and prepare:
                        bc_in(b + 1, f + F_BC)
                    if i == 7 and prepare:
                        dt_in(b + 1, 1, f + F_DT1)
                    if i < IN:
                        decay(b, i, 1)
                    if not (last and i >= STEPS - 3):
                        copy_x(s + 2)
                    if not (last and i == STEPS - 1):
                        weigh(s)
                    if i in (2, 3) and prepare:
                        conv_in(b + 1, i - 2, f + F_IN0 + i - 2)
                    if i == 5 and prepare:
                        conv_tanh(b + 1)
                    if i == 6 and prepare:
                        dt_in(b + 1, 0, f + F_DT0)
                    if i == 7 and prepare:
                        exp_dt(b + 1)

                conv_in(0, 0, 0)
                conv_in(0, 1, 1)
                copy_x(0)
                conv_tanh(0)
                for h in range(2):
                    tanh_h(0, h)
                copy_x(1)
                bc_in(0, 2)
                dt_in(0, 0, 3)
                dt_in(0, 1, 4)
                exp_dt(0)
                ln_dt(0)
                act.wait_ge(s_an, 2)
                for i in range(2):
                    step(0, i)
                with act.Fori(0, B - 1) as b:
                    for i in range(2, STEPS):
                        step(b, i)
                    for i in range(2):
                        step(b + 1, i)
                for i in range(2, STEPS):
                    step(B - 1, i, last=True)

            @block.vector
            def _(dve):
                dve.memset(xs[:, :, 0:TAPS - 1], 0.0).then_inc(s_an0, 1)
                for r in range(2):
                    dve.memset(da[:, r, :, 0], 0.0).then_inc(s_dafree, 1)
                dve.wait_ge(s_an, 1)
                dve.tensor_scalar(aneg, aneg, -1.0, None, ALU.mult).then_inc(s_an, 1)
                dve.wait_ge(s_an0, 1)

                def conv(b, m, f):
                    dve.wait_ge(s_ffree, f + 1)
                    w = C_CW + TAPS * m
                    at = b * 8 + 4 * m
                    dve.tensor_scalar(xc[:, m, :], xs[:, m, 0:L], col[:, w:w + 1], col[:, C_CB + m:C_CB + m + 1],
                                      ALU.mult, ALU.add).then_inc(s_tap, 1)
                    for t in range(1, TAPS):
                        dve.wait_ge(s_tap, at + t)
                        dve.scalar_tensor_tensor(xc[:, m, :], xs[:, m, t:t + L], col[:, w + t:w + t + 1], xc[:, m, :],
                                                 ALU.mult, ALU.add).then_inc(s_tap, 1)

                def gate(b, m):
                    dve.wait_ge(s_gt, b * KD + m + 1)
                    dve.scalar_tensor_tensor(gs[:, m, :], sp[:, m, :], 1.0, gs[:, m, :], ALU.add,
                                             ALU.mult).then_inc(s_gs, 1)

                def conv_act(b):
                    for m in range(KD):
                        dve.wait_ge(s_ct, b * KD + m + 1)
                        dve.scalar_tensor_tensor(xc[:, m, :], xsv[:, m, :], 1.0, xc[:, m, :], ALU.add,
                                                 ALU.mult).then_inc(s_xv, 1)

                def bc_parts(b, f):
                    dve.wait_ge(s_ffree, f + 1)
                    if positive(b):
                        dve.wait_ge(s_bcp, b)
                    dve.tensor_copy(bcnext[:, :], bcf).then_inc(s_part, 1)
                    dve.wait_ge(s_part, b * 5 + 1)
                    dve.tensor_tensor(bcf, bcf, bcnext[:, :], ALU.subtract).then_inc(s_part, 1)
                    dve.wait_ge(s_part, b * 5 + 2)
                    for r in (1, 2):
                        dve.tensor_copy(bcnext[32 * r:32 * r + 32, :], bcf[32 * r:32 * r + 32, :]).then_inc(s_part, 1)
                    dve.wait_ge(s_part, b * 5 + 4)
                    dve.tensor_tensor(bcnext[64:96, :], bcf[64:96, :], bcnext[64:96, :], ALU.subtract).then_inc(s_part, 1)

                def take_bc(b):
                    if positive(b):
                        dve.wait_ge(s_bcr, b * NST)
                    dve.wait_ge(s_part, b * 5 + 5)
                    dve.tensor_copy(bcpart[:, :], bcnext[:, :]).then_inc(s_bcp, 1)

                def inputs(b):
                    if positive(b):
                        dve.wait_ge(s_da, b * NST * KD)
                    dve.wait_ge(s_sp, b * 4 + 4)
                    dve.scalar_tensor_tensor(dtt[:, :, :], xsv, 0.0, sp[:, :, :], ALU.max, ALU.add).then_inc(s_dtt, 1)
                    dve.wait_ge(s_dtt, b + 1)
                    dve.scalar_tensor_tensor(u[:, :, :], xc, 0.5, dtt[:, :, :], ALU.mult, ALU.mult).then_inc(s_u, 1)

                def start_sum(b):
                    for m in range(KD):
                        dve.tensor_scalar(y[:, m, :], xc[:, m, :], dhalf[:, m:m + 1], None,
                                          ALU.mult).then_inc(s_y0, 1)

                def hidden(j, h):
                    dve.wait_ge(s_th, j * 2 + h + 1)
                    dve.scalar_tensor_tensor(th[:, h * 512:(h + 1) * 512], th[:, h * 512:(h + 1) * 512], 1.0,
                                             psum[f"up{h}"][:, :], ALU.add, ALU.mult).then_inc(s_hs, 1)

                def times_b(b, i, r):
                    g = b * NST + i * NU + r
                    if i == 0 and r == 0:
                        dve.wait_ge(s_u, b + 1)
                    dve.wait_ge(s_bb, g + 1)
                    if positive(g - 1):
                        dve.wait_ge(s_sum, g - 1)
                    dve.tensor_tensor(ring[:, r, :, :], u[:, :, :],
                                      psum["bb"][:, :].unsqueeze(1).to_broadcast([P, KD, L]),
                                      ALU.mult).then_inc(s_um, 1)

                def scan_c(b, i, r):
                    g = b * NST + i * NU + r
                    row = ring[:, r, :, :]
                    dve.wait_ge(s_um, g + 1)
                    dve.wait_ge(s_da, g * 2 + 2)
                    dve.tensor_tensor_scan(row.rearrange("p k l -> p (k l)"),
                                           da[:, r, :, :].rearrange("p k l -> p (k l)"),
                                           row.rearrange("p k l -> p (k l)"), 0.0, ALU.mult,
                                           ALU.add).then_inc(s_dafree, 1)
                    dve.wait_ge(s_dafree, g + 3)
                    dve.wait_ge(s_bcr, g + 1)
                    dve.tensor_tensor(row, row, psum["bc"][:, :].unsqueeze(1).to_broadcast([P, KD, L]),
                                      ALU.mult).then_inc(s_hc, 1)

                def gated(b):
                    dve.wait_ge(s_sum, (b + 1) * NST)
                    dve.wait_ge(s_gs, (b + 1) * KD)
                    dve.scalar_tensor_tensor(y[:, :, :], y[:, :, :], 0.5, gs[:, :, :], ALU.mult,
                                             ALU.mult).then_inc(s_yg, 1)

                def add_xn(b, f):
                    dve.wait_ge(s_xtok, b * 16 + 16)
                    dve.wait_ge(s_frdy, f + 1)
                    dve.tensor_tensor(xtok[:, 0:2, :], xtok[:, 0:2, :],
                                      psum["fr"][:, :].rearrange("p (j d) -> p j d", j=2), ALU.add).then_inc(s_ffree, 1)
                    dve.wait_ge(s_o1, b + 1)
                    dve.tensor_tensor(xtok[:, 2:4, :], xtok[:, 2:4, :],
                                      psum["bc"][:, :].rearrange("p (j d) -> p j d", j=2), ALU.add).then_inc(s_z1, 1)

                def statistics(b, f):
                    dve.wait_ge(s_ffree, f + 1)
                    dve.wait_ge(s_z1, b + 1)
                    for j in range(TB):
                        dve.bn_stats(stat[:, j, :], xtok[:, j, :]).then_inc(s_zs, 1)
                    counted = held(dve, b * TB + TB)
                    dve.wait_ge(s_an, 2)
                    dve.wait_ge(s_zs, counted)
                    for j in range(TB):
                        dve.bn_aggr(mv[:, j, :], stat[:, j, :]).then_inc(s_za, 1)

                def invert(b):
                    dve.wait_ge(s_za, b * TB + TB)
                    rsqrt(dve, rstd[:, :], mv[:, :, 1], rt_i[:, :], rt_t[:, :], s_zr, b * RSQ)

                def normalise(b):
                    for j in range(TB):
                        dve.tensor_scalar(xtok[:, j, :], xtok[:, j, :], mv[:, j, 0:1], rstd[:, j:j + 1],
                                          ALU.subtract, ALU.mult).then_inc(s_zn, 1)

                def step(b, i, prev=None, last=False):
                    s, f = b * STEPS + i, b * FS
                    prepare = not last
                    if i < IN:
                        times_b(b, i, 0)
                        scan_c(b, i, 0)
                        if not (last and i >= STEPS - 2):
                            hidden(s + 1, 0)
                            hidden(s + 1, 1)
                        times_b(b, i, 1)
                        scan_c(b, i, 1)
                    if i in (0, 1):
                        gate(b, i)
                    if prev is not None:
                        if i == 0:
                            statistics(prev, prev * FS + F_OUT)
                        if i == 1:
                            invert(prev)
                        if i == 2:
                            normalise(prev)
                    if i in (3, 4) and prepare:
                        conv(b + 1, i - 3, f + F_IN0 + i - 3)
                    if i == 5 and prepare:
                        conv_act(b + 1)
                    if i == 6 and prepare:
                        bc_parts(b + 1, f + F_BC)
                    if i == 8 and prepare:
                        take_bc(b + 1)
                        inputs(b + 1)
                        gated(b)
                        hidden(s + 1, 0)
                        hidden(s + 1, 1)
                        add_xn(b, f + F_OUT)
                        start_sum(b + 1)

                conv(0, 0, 0)
                conv(0, 1, 1)
                conv_act(0)
                for h in range(2):
                    hidden(0, h)
                bc_parts(0, 2)
                take_bc(0)
                inputs(0)
                start_sum(0)
                for i in range(3):
                    step(0, i)
                with dve.Fori(0, B - 1) as b:
                    for i in range(3, STEPS):
                        step(b, i)
                    for i in range(3):
                        step(b + 1, i, prev=b)
                for i in range(3, STEPS - 1):
                    step(B - 1, i, last=True)
                gated(B - 1)
                add_xn(B - 1, (B - 1) * FS + F_OUT_LAST)
                statistics(B - 1, (B - 1) * FS + F_OUT_LAST)
                invert(B - 1)
                normalise(B - 1)

            @block.tensor
            def _(pe):
                def project(at, rows_out, f, src):
                    if positive(f):
                        pe.wait_ge(s_ffree, f)
                    for k in range(KD):
                        mm = pe.matmul(psum["fr"][0:rows_out, :], wm[:, k, at:at + rows_out], src[:, k, :],
                                       start=(k == 0), stop=(k == KD - 1))
                    mm.then_inc(s_frdy, 1)

                def proj_in(b, m, f):
                    if m == 0:
                        pe.wait_ge(s_xnt, b * 16 + 16)
                    project(W_IN + m * P, P, f, xnt)

                def proj_bc(b, f):
                    pe.wait_ge(s_xv, b * KD + KD)
                    project(W_BC, PARTS, f, xc)

                def proj_dt(m, f):
                    project(W_DT + m * P, P, f, xc)

                def proj_out(b, f):
                    pe.wait_ge(s_yg, b + 1)
                    pe.wait_ge(s_ffree, f)
                    for o, (bank, ready) in enumerate((("fr", s_frdy), ("bc", s_o1))):
                        for c in range(2):
                            j = 2 * o + c
                            dst = psum[bank][:, c * D:(c + 1) * D]
                            pe.matmul(dst, sel[:, E:E + 1].to_broadcast([PARTS, P]), bpart[:, H:BW],
                                      start=True, stop=False)
                            for k in range(KD):
                                mm = pe.matmul(dst, y[:, k, j * P:(j + 1) * P], wm[:, k, W_OUT:W_OUT + D],
                                               start=False, stop=(k == KD - 1))
                        mm.then_inc(ready, 1)

                def spread_b(b, i, r):
                    g, n = b * NST + i * NU + r, i * NU + r
                    if i == 0 and r == 0:
                        pe.wait_ge(s_bcp, b + 1)
                    if positive(g):
                        pe.wait_ge(s_um, g)
                    pe.matmul(psum["bb"][:, :], sel[:, n:n + 1].to_broadcast([PARTS, P]), bcpart[:, :],
                              start=True, stop=True).then_inc(s_bb, 1)

                def spread_c(b, i, r):
                    g, n = b * NST + i * NU + r, i * NU + r + NST
                    if positive(g):
                        pe.wait_ge(s_hc, g)
                        if i == 0 and r == 0:
                            pe.wait_ge(s_z1, b)
                    pe.matmul(psum["bc"][:, :], sel[:, n:n + 1].to_broadcast([PARTS, P]), bcpart[:, :],
                              start=True, stop=True).then_inc(s_bcr, 1)

                def turn_x(j):
                    pe.wait_ge(s_xg, j * 16 + 16)
                    if positive(j - 1):
                        pe.wait_ge(s_ht, j * 2 - 2)
                    for k in range(KD):
                        mm = pe.transpose(tr_x[:, k * P:(k + 1) * P], xg[:, k * P:(k + 1) * P], ident[:, :])
                    mm.then_inc(s_xtr, 1)

                def expert(j):
                    return pe.value_load(te_i[0:1, bass.ds(j, 1)], min_val=0, max_val=E - 1)

                def up(j, e, h):
                    if h == 0:
                        pe.wait_ge(s_xtc, j + 1)
                        if positive(j):
                            pe.wait_ge(s_hs, j * 2)
                    cs = slice(h * 512, (h + 1) * 512)
                    pe.matmul(psum[f"up{h}"][:, :], sel[:, bass.ds(e, 1)].to_broadcast([PARTS, P]), bpart[:, cs],
                              start=True, stop=False)
                    for k in range(KD):
                        mm = pe.matmul(psum[f"up{h}"][:, :], xgt[:, k, :], w1[:, bass.ds(e, 1), k, cs],
                                       start=False, stop=(k == KD - 1))
                    mm.then_inc(s_up, 1)

                def turn_h(j, followed=True):
                    for h in range(2):
                        if h == 0 and positive(j):
                            pe.wait_ge(s_ht, j * 2)
                        if h == 1 and followed:
                            pe.wait_ge(s_xtc, j + 2)
                        pe.wait_ge(s_hs, j * 2 + h + 1)
                        for c in range(4):
                            at = (4 * h + c) * P
                            mm = pe.transpose(psum[f"tr{h}"][:, c * P:(c + 1) * P], th[:, at:at + P], ident[:, :])
                        mm.then_inc(s_t, 1)

                def down(j, e, half):
                    if half == 0:
                        pe.wait_ge(s_ht, j * 2 + 2)
                        if positive(j):
                            pe.wait_ge(s_y, j)
                        pe.matmul(yx_y, sel[:, bass.ds(e, 1)].to_broadcast([PARTS, P]), bpart[:, H:BW],
                                  start=True, stop=False)
                    for k in range(half * KH // 2, (half + 1) * KH // 2):
                        mm = pe.matmul(yx_y, ht[:, k, :], w2[:, bass.ds(e, 1), k, :], start=False, stop=(k == KH - 1))
                    if half == 1:
                        mm.then_inc(s_dn, 1)

                def step(b, i, last=False):
                    s, f = b * STEPS + i, b * FS
                    prepare = not last
                    first_layer = not (last and i >= STEPS - 2)
                    second_layer = not (last and i == STEPS - 1)
                    if first_layer:
                        e = expert(s + 1)
                    if i < IN:
                        spread_b(b, i, 0)
                    if first_layer:
                        up(s + 1, e, 0)
                    if i < IN:
                        spread_c(b, i, 0)
                    if i in (0, 1):
                        proj_in(b, KD + i, f + F_G0 + i)
                    if i in (2, 3) and prepare:
                        proj_in(b + 1, i - 2, f + F_IN0 + i - 2)
                    if i == 6 and prepare:
                        proj_bc(b + 1, f + F_BC)
                    if i == 7 and prepare:
                        proj_dt(1, f + F_DT1)
                    if first_layer:
                        up(s + 1, e, 1)
                    if second_layer:
                        e = expert(s)
                    if second_layer:
                        down(s, e, 0)
                    if i < IN:
                        spread_b(b, i, 1)
                    if second_layer:
                        if not (last and i >= STEPS - 3):
                            turn_x(s + 2)
                        down(s, e, 1)
                    if i == 6 and prepare:
                        proj_dt(0, f + F_DT0)
                    if i < IN:
                        spread_c(b, i, 1)
                    if i == 8:
                        proj_out(b, f + (F_OUT_LAST if last else F_OUT))
                    if first_layer:
                        turn_h(s + 1, followed=not (last and i >= STEPS - 3))

                proj_in(0, 0, 0)
                proj_in(0, 1, 1)
                turn_x(0)
                pe.wait_ge(s_brd, 2)
                pe.wait_ge(s_w, 16 * 2 * E)
                e = expert(0)
                for h in range(2):
                    up(0, e, h)
                turn_x(1)
                turn_h(0)
                proj_bc(0, 2)
                proj_dt(0, 3)
                proj_dt(1, 4)
                for i in range(2):
                    step(0, i)
                with pe.Fori(0, B - 1) as b:
                    for i in range(2, STEPS):
                        step(b, i)
                    for i in range(2):
                        step(b + 1, i)
                for i in range(2, STEPS):
                    step(B - 1, i, last=True)
    return nc


_ORDER = ("x", "cols", "rows", "wmix", "wroute", "brows", "we1", "we2", "consts", "constb")


def kernel(**inputs):
    import ml_dtypes
    import numpy as np
    import concourse.bacc as bacc
    from concourse.bass_utils import run_bass_kernel_spmd

    a = {k[3:]: np.asarray(v) for k, v in inputs.items()}

    def by_part(v):
        return v.reshape(-1, P).T

    def rows_of(w):
        return w.reshape(KD, P, -1).transpose(1, 0, 2)

    bcb = np.concatenate([a["attn_bc_b"]] * 3 + [np.zeros(P - PARTS, np.float32)])
    bcw = a["attn_bc_w"].T
    brows = np.zeros((32, BW), np.float32)
    brows[0:E, 0:H] = a["ffn_be1"]
    brows[0:E, H:BW] = a["ffn_be2"]
    brows[E, H:BW] = a["attn_out_b"]
    lay = {
        "x": a["attn_x"].reshape(TOK, D),
        "cols": np.concatenate([by_part(a["attn_in_proj_b"]), a["attn_conv_w"].reshape(KD, P, TAPS).transpose(1, 0, 2).reshape(P, -1),
                                by_part(a["attn_conv_b"]), by_part(a["attn_dt_b"]), by_part(a["attn_D"]),
                                a["attn_A_log"].reshape(KD, P, NST).transpose(1, 0, 2).reshape(P, -1),
                                by_part(a["ffn_rb1"]), by_part(bcb)], axis=1),
        "rows": np.concatenate([a["attn_ln_g"], a["attn_ln_b"], a["ffn_rb2"]]),
        "wmix": rows_of(np.concatenate([a["attn_in_proj_w"].T, bcw, bcw, bcw, a["attn_dt_w"].T, a["attn_out_w"].T], axis=1)),
        "wroute": rows_of(np.concatenate([a["ffn_rw1"], a["ffn_rw2"]], axis=1)),
        "brows": brows,
        "we1": a["ffn_we1"],
        "we2": a["ffn_we2"],
    }
    p = np.arange(P, dtype=np.float32)
    one = np.ones((P, 1), np.float32)
    reset = (np.arange(E * TT) % TT != 0).astype(np.float32)
    lay["consts"] = np.concatenate([
        np.eye(P, dtype=np.float32), one * p, one * np.arange(MC, dtype=np.float32),
        one * (P * np.arange(TT, dtype=np.float32)), one * reset,
        p[:, None] + P * np.arange(TT, dtype=np.float32) - TOK, p[:, None] + TOK], axis=1)
    lay["constb"] = np.concatenate([p[:, None] < p, np.ones((P, P), bool), p[:, None] % 32 == np.arange(32)],
                                   axis=1).astype(ml_dtypes.bfloat16)

    nc = bacc.Bacc("TRN2", target_bir_lowering=False, num_devices=1)
    arrays, args = {}, []
    for name in _ORDER:
        v = np.ascontiguousarray(lay[name])
        arrays[f"in_{name}"] = v
        args.append(nc.dram_tensor(f"in_{name}", v.shape, mybir.dt.from_np(v.dtype), kind="ExternalInput").ap())
    res = nc.dram_tensor("out_0", (TOK, D), F32, kind="ExternalOutput").ap()
    build(nc, *args, res)
    r = run_bass_kernel_spmd(nc, [arrays], core_ids=[0])
    return r.results[0]["out_0"].reshape(B, L, D)
```

```python
from contextlib import ExitStack

import concourse.bass as bass
from concourse import mybir
from concourse.alu_op_type import AluOpType as ALU

ACT = mybir.ActivationFunctionType
AX = mybir.AxisListType
F32 = mybir.dt.float32
BF16 = mybir.dt.bfloat16
I32 = mybir.dt.int32

P = 128
B, L, D = 8, 512, 256
KD = D // P
NST, TAPS = 16, 4
E, H, TOPK = 8, 1024, 2
KH = H // P
TOK = B * L
TT = TOK // P
TB = L // P
EPS = 1e-5
MT = TOPK * TOK // P + E - 1
STEPS = 9
assert STEPS * B - 1 == MT
MC = MT + 3
PARTS = 96
BW = H + D

C_INB, C_CW, C_CB, C_DTB, C_D, C_AL, C_RB1, C_BCB, NCOL = 0, 4, 12, 14, 16, 18, 50, 52, 53
W_IN, W_BC, W_DT, W_OUT, NW = 0, 512, 608, 864, 1120
K_ID, K_IOTA, K_J, K_128, K_RST, K_TOK, K_PAD, NK = 0, 128, 256, 256 + MC, 288 + MC, 544 + MC, 576 + MC, 577 + MC


def held(eng, value):
    return value if isinstance(value, int) else eng.to_reg(value)


def build(nc, x, cols, rows, wmix, wroute, brows, we1, we2, consts, constb, out):
    ctx = ExitStack()
    with ctx:
        def sb(name, shape, dt=F32):
            return ctx.enter_context(nc.sbuf_tensor(name, shape, dt))

        def sem(name):
            return ctx.enter_context(nc.semaphore(name))

        psum = {n: ctx.enter_context(nc.psum_tensor("ps_" + n, [P, 512], F32))
                for n in ("up0", "up1", "tr0", "tr1", "yx", "bb", "bc", "fr")}

        xn_d = nc.dram_tensor("xn_scratch", [TOK, D], F32, kind="Internal").ap()
        xnt_d = nc.dram_tensor("xnt_scratch", [B * P, KD * L], F32, kind="Internal").ap()

        w1 = sb("w1", [P, E, KD, H])
        w2 = sb("w2", [P, E, KH, D])
        wm = sb("wm", [P, KD, NW])
        col = sb("col", [P, NCOL])
        dhalf = sb("dhalf", [P, KD])
        aneg = col[:, C_AL:C_AL + KD * NST].rearrange("p (k n) -> p k n", k=KD)
        gam = sb("gam", [P, D])
        ident = sb("ident", [P, P])
        sel = sb("sel", [PARTS, 32], BF16)
        bpart = sb("bpart", [PARTS, BW], BF16)
        bcpart = sb("bcpart", [PARTS, L], BF16)
        bcnext = sb("bcnext", [PARTS, L], BF16)
        te_i = sb("te_i", [P, MC], I32)
        gid = sb("gid", [P, MC], I32)
        sid = sb("sid", [P, MC], I32)
        wslot = sb("wslot", [P, MC])
        gcur = sb("gcur", [P, 1], I32)
        scur = sb("scur", [P, 1], I32)
        stat = sb("stat", [P, TB, 6])
        mv = sb("mv", [P, TB, 2])
        rstd = sb("rstd", [P, TB])
        ring = sb("ring", [P, 2, KD, L])
        da = sb("da", [P, 2, KD, L])
        xx = sb("xx", [P, 2, KD, L])
        xnt, xc = xx[:, 0, :, :], xx[:, 1, :, :]
        gd = sb("gd", [P, 2, KD, L])
        gs, dtt = gd[:, 0, :, :], gd[:, 1, :, :]
        u = sb("u", [P, KD, L])
        xs = sb("xs", [P, KD, L + TAPS - 1])
        sp = sb("sp", [P, KD, L])
        y = sb("y", [P, KD, L])
        xtok = sb("xtok", [P, TB, D])
        xg = sb("xg", [P, D])
        xgt = sb("xgt", [P, KD, P])
        th = sb("th", [P, H])
        ht = sb("ht", [P, KH, P])
        yo = sb("yo", [P, D])

        rt_i = sb("rt_i", [P, TB], I32)
        scrap = sb("scrap", [P, 1])
        rt_t = sb("rt_t", [P, TB])
        RSQ = 12

        def rsqrt(dve, res, var, ti, tf, done, c):
            dve.tensor_scalar(var, var, EPS, None, ALU.add).then_inc(done, 1)
            dve.wait_ge(done, c + 1)
            dve.tensor_single_scalar(ti, var.bitcast(I32), 1, ALU.logical_shift_right).then_inc(done, 1)
            dve.wait_ge(done, c + 2)
            dve.tensor_scalar(res.bitcast(I32), ti, -1.0, float(0x5F3759DF), ALU.mult, ALU.add).then_inc(done, 1)
            for step in range(3):
                dve.wait_ge(done, c + 3 + 3 * step)
                dve.tensor_tensor(tf, res, res, ALU.mult).then_inc(done, 1)
                dve.wait_ge(done, c + 4 + 3 * step)
                dve.scalar_tensor_tensor(tf, tf, -0.5, var, ALU.mult, ALU.mult).then_inc(done, 1)
                dve.wait_ge(done, c + 5 + 3 * step)
                dve.scalar_tensor_tensor(res, tf, 1.5, res, ALU.add, ALU.mult).then_inc(done, 1)
            dve.wait_ge(done, c + RSQ)

        s_const = sem("s_const")
        s_w = sem("s_w")

        def flat(a):
            return a.rearrange("p k l -> p (k l)")

        xall = w2.rearrange("p e k d -> p (e k) d")[:, 0:TT, :]
        xnb = [da[:, q, :, :].rearrange("p k (j f) -> p (k j) f", j=2) for q in range(2)]
        head = flat(sp[:, :, :])
        stat1 = head[:, 0:6 * TT].rearrange("p (t s) -> p t s", s=6)
        mv1 = head[:, 6 * TT:8 * TT].rearrange("p (t s) -> p t s", s=2)
        rstd1, tf1 = head[:, 8 * TT:9 * TT], head[:, 9 * TT:10 * TT]
        ti1 = head[:, 10 * TT:11 * TT].bitcast(I32)
        rowb = flat(sp[:, :, :])[:, 384:384 + D + E]
        ks = flat(u[:, :, :])[:, 0:NK - P]
        tri = flat(u[:, :, :])[:, NK - P:NK - P + P // 2].bitcast(BF16)
        ones = flat(u[:, :, :])[:, NK - P // 2:NK].bitcast(BF16)
        spare = w2.rearrange("p e k d -> p (e k d)")[0:PARTS, (E - 1) * KH * D:(E - 1) * KH * D + BW]
        stage0, stage1 = spare[:, 0:H], spare[:, H:BW]
        xtb = [xnt, xc]
        rv = [gs, dtt]
        rt = y
        wr = th[:, 0:KD * 264].rearrange("p (k n) -> p k n", k=KD)
        logit = xtok[:, 0, :].rearrange("p (t e) -> p t e", e=E)
        x_v = x.rearrange("(b j p) d -> b p j d", p=P, j=TB)
        xn_v = xn_d.rearrange("(b j p) d -> b p j d", p=P, j=TB)
        out_v = out.rearrange("(b j p) d -> b p j d", p=P, j=TB)
        xnt_v = xnt_d.rearrange("(b p) (k l) -> b p k l", p=P, k=KD)

        s_l2 = sem("s_l2")
        nslot_big = xtok[:, :, :].rearrange("p j f -> p (j f)")[:, 0:E * MC]
        XP = 4
        s_x = [sem(f"s_x{q}") for q in range(XP)]
        s_st = sem("s_st")
        s_ag = sem("s_ag")
        s_rs = sem("s_rs")
        s_xn = sem("s_xn")
        s_res = sem("s_res")
        s_xnw = [sem(f"s_xnw{q}") for q in range(2)]
        s_acc = sem("s_acc")
        s_xtw = [sem(f"s_xtw{q}") for q in range(2)]
        s_wm = sem("s_wm")
        s_k2 = sem("s_k2")
        s_brow = sem("s_brow")
        s_pb = sem("s_pb")
        s_brd = sem("s_brd")
        s_tr = sem("s_tr")
        s_xt = sem("s_xt")
        s_rm = sem("s_rm")
        s_rv = sem("s_rv")
        s_rt = sem("s_rt")
        s_rs2 = sem("s_rs2")
        s_lg = sem("s_lg")
        s_lg2 = sem("s_lg2")
        s_const2 = sem("s_const2")
        s_scaled = sem("s_scaled")

        with nc.Block() as block:
            @block.sync
            def _(sync):
                for piece in range(XP):
                    n = TT // XP
                    sync.dma_start(xall[:, piece * n:(piece + 1) * n, :],
                                   x.rearrange("(t p) d -> p t d", p=P)[:, piece * n:(piece + 1) * n, :]
                                   ).then_inc(s_x[piece], 16)

                def store(h, q):
                    sync.wait_ge(s_xn, h * 8 + 4 * q + 4)
                    sync.dma_start(xn_v[h * 2 + q], xnb[q]).then_inc(s_xnw[q], 16)
                    sync.wait_ge(s_xt, h * 4 + 2 * q + 2)
                    sync.dma_start(xnt_v[h * 2 + q], xtb[q]).then_inc(s_xtw[q], 16)

                with sync.Fori(0, B // 2) as i:
                    for q in range(2):
                        store(i, q)

            @block.gpsimd
            def _(pool):
                for r in range(3):
                    pool.dma_start(spare[32 * r:32 * r + 32, :], brows).then_inc(s_brow, 16)
                with pool.Fori(0, B // 2) as i:
                    for q in range(2):
                        n = i * 2 + q
                        xa = xall[:, bass.ts(n, TB), :]
                        normed = held(pool, n * 4 + 4)
                        pool.wait_ge(s_brow, 48)
                        pool.wait_ge(s_xn, normed)
                        pool.tensor_tensor(xa, xa, xnb[q], ALU.add).then_inc(s_res, 1)
                        pool.wait_ge(s_res, n + 1)
                        pool.dma_start(out_v[n], xa).then_inc(s_acc, 16)

            @block.vector
            def _(dve):
                def statistics(n):
                    if n % 2 == 0:
                        dve.wait_ge(s_x[n // 2], 16)
                    for t in range(n * TB, n * TB + TB):
                        dve.bn_stats(stat1[:, t, :], xall[:, t, :]).then_inc(s_st, 1)
                    dve.wait_ge(s_st, n * TB + TB)
                    for t in range(n * TB, n * TB + TB):
                        dve.bn_aggr(mv1[:, t, :], stat1[:, t, :]).then_inc(s_ag, 1)

                def invert(piece):
                    at = slice(piece * 2 * TB, (piece + 1) * 2 * TB)
                    dve.wait_ge(s_ag, (piece + 1) * 2 * TB)
                    rsqrt(dve, rstd1[:, at], mv1[:, at, 1], ti1[:, at], tf1[:, at], s_rs, piece * RSQ)

                def norm(h, q):
                    if h > 0:
                        dve.wait_ge(s_xnw[q], h * 16)
                        dve.wait_ge(s_tr, (h * 2 + q) * 2 - 2)
                        dve.wait_ge(s_res, h * 2 + q - 1)
                    for j in range(TB):
                        t = (h * 2 + q) * TB + j
                        dve.tensor_scalar(xnb[q][:, j, :], xall[:, t, :], mv1[:, t, 0:1], rstd1[:, t:t + 1], ALU.subtract, ALU.mult).then_inc(s_xn, 1)

                def hidden(h, q):
                    for m in range(KD):
                        dve.wait_ge(s_rt, h * 4 + 2 * q + m + 1)
                        dve.scalar_tensor_tensor(rv[q][:, m, :], rt[:, m, :], 1.0, rv[q][:, m, :],
                                                 ALU.add, ALU.mult).then_inc(s_rs2, 1)

                statistics(0)
                statistics(1)
                invert(0)
                norm(0, 0)
                norm(0, 1)
                statistics(2)
                statistics(3)
                invert(1)
                dve.wait_ge(s_const, 48)
                dve.tensor_scalar(wr[:, :, 256:264], wr[:, :, 256:264], 0.5, None, ALU.mult).then_inc(s_scaled, 1)
                dve.tensor_scalar(dhalf[:, :], col[:, C_D:C_D + KD], 0.5, None, ALU.mult).then_inc(s_scaled, 1)
                for i in range(B // 2 - 1):
                    norm(i + 1, 0)
                    hidden(i, 0)
                    if i + 2 < XP:
                        statistics(2 * i + 4)
                    norm(i + 1, 1)
                    hidden(i, 1)
                    if i + 2 < XP:
                        statistics(2 * i + 5)
                        invert(i + 2)
                dve.wait_ge(s_wm, 16)
                dve.tensor_scalar(wm[:, :, W_BC:W_OUT], wm[:, :, W_BC:W_OUT], 0.5, None, ALU.mult).then_inc(s_scaled, 1)
                hidden(B // 2 - 1, 0)
                hidden(B // 2 - 1, 1)

            @block.tensor
            def _(pe):
                def turn(h, q):
                    pe.wait_ge(s_xn, h * 8 + 4 * q + 4)
                    pe.wait_ge(s_xt, h * 4 + 2 * q)
                    for k in range(KD):
                        ps = psum[f"up{k}"]
                        for j in range(TB):
                            mm = pe.transpose(ps[:, j * P:(j + 1) * P], xnb[q][:, j, k * P:(k + 1) * P], ident[:, :])
                        mm.then_inc(s_tr, 1)

                def route(h, q):
                    pe.wait_ge(s_xt, h * 4 + 2 * q + 2)
                    pe.wait_ge(s_rv, h * 4 + 2 * q)
                    for m in range(KD):
                        for k in range(KD):
                            mm = pe.matmul(psum[f"tr{m}"][:, :], wr[:, k, m * P:(m + 1) * P], xtb[q][:, k, :],
                                           start=(k == 0), stop=(k == KD - 1))
                        mm.then_inc(s_rm, 1)

                def logits(h, q):
                    pe.wait_ge(s_rs2, h * 4 + 2 * q + 2)
                    pe.wait_ge(s_lg, h * 2 + q)
                    for j in range(TB):
                        for k in range(KD):
                            mm = pe.matmul(psum["yx"][:, j * E:(j + 1) * E], rv[q][:, k, j * P:(j + 1) * P],
                                           wr[:, k, 256:264], start=(k == 0), stop=(k == KD - 1))
                    mm.then_inc(s_lg2, 1)

                pe.wait_ge(s_const, 48)
                turn(0, 0)
                turn(0, 1)
                route(0, 0)
                pe.wait_ge(s_scaled, 1)
                with pe.Fori(0, B // 2 - 1) as i:
                    turn(i + 1, 0)
                    route(i, 1)
                    logits(i, 0)
                    turn(i + 1, 1)
                    route(i + 1, 0)
                    logits(i, 1)
                route(B // 2 - 1, 1)
                logits(B // 2 - 1, 0)
                logits(B // 2 - 1, 1)

            @block.scalar
            def _(act):
                act.dma_start(ident[:, :], consts[:, K_ID:K_ID + P]).then_inc(s_const, 16)
                act.dma_start(wr, wroute).then_inc(s_const, 16)
                act.dma_start(col[:, :], cols).then_inc(s_const, 16)
                act.dma_start(gam[:, :], rows[0:D].partition_broadcast(P)).then_inc(s_const2, 16)
                act.dma_start(rowb, rows[D:2 * D + E].partition_broadcast(P)).then_inc(s_const2, 16)
                act.dma_start(sel[:, :], constb[0:PARTS, 2 * P:2 * P + 32]).then_inc(s_const2, 16)
                act.dma_start(wm[:, :, :], wmix).then_inc(s_wm, 16)
                act.dma_start(ks, consts[:, P:NK]).then_inc(s_k2, 16)
                act.dma_start(flat(u[:, :, :])[:, NK - P:NK].bitcast(BF16), constb[:, 0:2 * P]).then_inc(s_k2, 16)

                def copy_xt(h, q):
                    act.wait_ge(s_xtw[q], h * 16)
                    for k in range(KD):
                        act.wait_ge(s_tr, h * 4 + 2 * q + k + 1)
                        act.activation(xtb[q][:, k, :], psum[f"up{k}"][:, :], ACT.Copy).then_inc(s_xt, 1)

                def hidden(h, q):
                    act.wait_ge(s_rs2, h * 4 + 2 * q)
                    for m in range(KD):
                        act.wait_ge(s_rm, h * 4 + 2 * q + m + 1)
                        act.activation(rv[q][:, m, :], psum[f"tr{m}"][:, :], ACT.Identity,
                                       bias=col[:, C_RB1 + m:C_RB1 + m + 1]).then_inc(s_rv, 1)
                        act.wait_ge(s_rv, h * 4 + 2 * q + m + 1)
                        act.activation(rt[:, m, :], rv[q][:, m, :], ACT.Tanh, scale=0.5).then_inc(s_rt, 1)

                def copy_logits(h, q):
                    act.wait_ge(s_lg2, h * 2 + q + 1)
                    act.activation(logit[:, bass.ts(h * 2 + q, TB), :],
                                   psum["yx"][:, 0:TB * E].rearrange("p (j e) -> p j e", e=E),
                                   ACT.Copy).then_inc(s_lg, 1)

                act.wait_ge(s_const, 48)
                copy_xt(0, 0)
                copy_xt(0, 1)
                hidden(0, 0)
                with act.Fori(0, B // 2 - 1) as i:
                    copy_xt(i + 1, 0)
                    hidden(i, 1)
                    copy_logits(i, 0)
                    copy_xt(i + 1, 1)
                    hidden(i + 1, 0)
                    copy_logits(i, 1)
                hidden(B // 2 - 1, 1)
                copy_logits(B // 2 - 1, 0)
                copy_logits(B // 2 - 1, 1)

        smalls = [flat(y[:, :, :])[:, i * 256:(i + 1) * 256] for i in range(4)] + \
                 [xtok[:, i, :] for i in range(1, 4)] + [flat(ht[:, :, :])[:, i * 256:(i + 1) * 256] for i in range(4)]
        et = [a.rearrange("p (e t) -> p e t", e=E) for a in smalls]
        lg, rank, beats, top0, top1, incl, slot, tmp, nslot = et[:9]
        k_iota, k_j = ks[:, K_IOTA - P:K_J - P], ks[:, K_J - P:K_128 - P]
        k_128, k_rst = ks[:, K_128 - P:K_RST - P], ks[:, K_RST - P:K_TOK - P]
        k_tok, k_pad = ks[:, K_TOK - P:K_PAD - P], ks[:, K_PAD - P:NK - P]
        both = th[:, P:2 * P].bitcast(BF16)
        KT = TOPK * TT
        pv = th[:, 256:1024].rearrange("p (n c) -> p n c", c=KT)
        slotf, af, bf, idv, wv, l01, e2 = (pv[:, i, :] for i in range(7))
        sloti, ai, bi = (pv[:, i, :].bitcast(I32) for i in range(7, 10))
        em = pv[:, 10, :]
        cnt, nt, sinc, st = em[:, 0:8], em[:, 8:16], em[:, 16:24], em[:, 24:32]
        st128, unit = em[:, 32:40], em[:, 40:48]
        CH = 8
        NCH = KT // CH
        ob = [ring[:, q, :, :].rearrange("p k (a c) -> p (k a) c", c=P) for q in range(2)]
        pair = [a.rearrange("p b k l -> p (b k l)") for a in (da[:, :, :, :], gd[:, :, :, :])]
        oa = [a[:, 2 * CH * MC:3 * CH * MC].rearrange("p (a c) -> p a c", c=MC) for a in pair]
        ov = [a[:, 0:2 * CH * MC].rearrange("p (a v c) -> p a v c", v=2, c=MC) for a in pair]

        s_dch = sem("s_dch")
        s_l = sem("s_l")
        s_e2 = sem("s_e2")
        s_both = sem("s_both")
        s_cum = sem("s_cum")
        s_val = sem("s_val")
        s_ob = sem("s_ob")
        s_oi = [sem(f"s_oi{q}") for q in range(2)]
        s_oa = sem("s_oa")
        s_ov = sem("s_ov")
        s_idm = sem("s_idm")
        s_tab = sem("s_tab")

        s_sum = sem("s_sum")
        s_dafree = sem("s_dafree")
        s_an = sem("s_an")
        s_an0 = sem("s_an0")
        s_xnt = sem("s_xnt")
        s_xtok = sem("s_xtok")
        s_frdy = sem("s_frdy")
        s_ffree = sem("s_ffree")
        s_gt = sem("s_gt")
        s_gs = sem("s_gs")
        s_tap0 = sem("s_tap0")
        s_tap = sem("s_tap")
        s_nb = sem("s_nb")
        s_ct = sem("s_ct")
        s_xv = sem("s_xv")
        s_part = sem("s_part")
        s_bcf = sem("s_bcf")
        s_bcp = sem("s_bcp")
        s_sp = sem("s_sp")
        s_v = sem("s_v")
        s_dtt = sem("s_dtt")
        s_u = sem("s_u")
        s_y0 = sem("s_y0")
        s_yg = sem("s_yg")
        s_o1 = sem("s_o1")
        s_z1 = sem("s_z1")
        s_bb = sem("s_bb")
        s_bcr = sem("s_bcr")
        s_um = sem("s_um")
        s_da = sem("s_da")
        s_hc = sem("s_hc")
        s_zs = sem("s_zs")
        s_za = sem("s_za")
        s_zr = sem("s_zr")
        s_zn = sem("s_zn")
        s_zg = sem("s_zg")
        s_gc = sem("s_gc")
        s_sc = sem("s_sc")
        s_xg = sem("s_xg")
        s_xtr = sem("s_xtr")
        s_xtc = sem("s_xtc")
        s_up = sem("s_up")
        s_th = sem("s_th")
        s_hs = sem("s_hs")
        s_t = sem("s_t")
        s_ht = sem("s_ht")
        s_dn = sem("s_dn")
        s_y = sem("s_y")
        s_sct = sem("s_sct")

        CT = KD * (TAPS - 1)
        IN = 8
        NU = NST // IN
        xsv = xs[:, :, TAPS - 1:]
        bcf = sp[0:PARTS, 1, :]
        yx_y, tr_x = psum["yx"][:, 0:D], psum["tr1"][:, 0:D]
        F_G0, F_G1, F_IN0, F_IN1, F_BC, F_DT0, F_DT1, F_OUT = range(5, 13)
        FS = 8
        F_OUT_LAST = F_OUT - 5

        def positive(n):
            return not isinstance(n, int) or n > 0

        with nc.Block() as block:
            @block.sync
            def _(sync):
                def load_xnt(b):
                    sync.wait_ge(s_frdy, b * FS - FS + F_G1 + 1)
                    sync.dma_start(xnt, xnt_v[b]).then_inc(s_xnt, 16)

                def load_xtok(b):
                    sync.wait_ge(s_acc, (b + B) * 16)
                    sync.dma_start(xtok[:, :, :], xn_v[b]).then_inc(s_xtok, 16)

                for q in range(2):
                    sync.wait_ge(s_xtw[q], 16 * B // 2)
                sync.dma_start(xnt, xnt_v[0]).then_inc(s_xnt, 16)
                for e in range(E):
                    if e == E - 1:
                        sync.wait_ge(s_brd, 2)
                    sync.dma_start(w1[:, e, :, :], we1[e].rearrange("(k p) h -> p k h", p=P)).then_inc(s_w, 16)
                    if e == 0:
                        sync.wait_ge(s_acc, 16 * B)
                    sync.dma_start(w2[:, e, :, :], we2[e].rearrange("(k p) d -> p k d", p=P)).then_inc(s_w, 16)
                sync.wait_ge(s_tab, 2)
                sync.dma_start(xtok[:, :, :], xn_v[0]).then_inc(s_xtok, 16)
                load_xnt(1)
                with sync.Fori(0, B - 2) as b:
                    load_xnt(b + 2)
                    load_xtok(b + 1)
                load_xtok(B - 1)

            @block.gpsimd
            def _(pool):
                def gather(j):
                    if positive(j):
                        pool.wait_ge(s_xg, j * 16)
                    pool.tensor_copy(gcur[:, :], gid[:, bass.ds(j, 1)]).then_inc(s_gc, 1)
                    this, last = held(pool, j + 1), held(pool, j)
                    pool.wait_ge(s_tab, 2)
                    pool.wait_ge(s_gc, this)
                    if positive(j):
                        pool.wait_ge(s_xtr, last)
                    pool.indirect_dma_start(xg[:, :], None, xn_d[:, :],
                                            bass.IndirectOffsetOnAxis(ap=gcur[:, :], axis=0)).then_inc(s_xg, 16)

                def scatter(s, b, i):
                    if positive(s):
                        pool.wait_ge(s_sct, s * 16)
                    if i == 4:
                        pool.wait_ge(s_acc, (b + B) * 16)
                    pool.tensor_copy(scur[:, :], sid[:, bass.ds(s, 1)]).then_inc(s_sc, 1)
                    this = held(pool, s + 1)
                    pool.wait_ge(s_tab, 2)
                    pool.wait_ge(s_sc, this)
                    pool.wait_ge(s_y, this)
                    pool.indirect_dma_start(out[:, :], bass.IndirectOffsetOnAxis(ap=scur[:, :], axis=0), yo[:, :], None,
                                            bounds_check=TOK - 1, oob_is_err=False,
                                            compute_op=ALU.add).then_inc(s_sct, 16)

                def add_state(b, i, r):
                    g = b * NST + i * NU + r
                    if i == 0 and r == 0:
                        pool.wait_ge(s_y0, (b + 1) * KD)
                    if positive(g):
                        pool.wait_ge(s_sum, g)
                    pool.wait_ge(s_hc, g + 1)
                    pool.tensor_tensor(y[:, :, :], y[:, :, :], ring[:, r, :, :], ALU.add).then_inc(s_sum, 1)

                def finish(b):
                    pool.wait_ge(s_zn, (b + 1) * TB)
                    pool.tensor_tensor(xtok[:, :, :], xtok[:, :, :],
                                       gam[:, :].unsqueeze(1).to_broadcast([P, TB, D]), ALU.mult).then_inc(s_zg, 1)

                def add_out(b, tiles, scaled):
                    pool.wait_ge(s_sct, tiles * 16)
                    pool.wait_ge(s_zg, scaled)
                    pool.dma_start(out_v[b], xtok[:, :, :], accum_op=ALU.add).then_inc(s_acc, 16)

                def step(b, i, prev=None, last=False):
                    s = b * STEPS + i
                    if i < IN:
                        add_state(b, i, 0)
                    if not (last and i >= STEPS - 4):
                        gather(s + 3)
                    if not (last and i == STEPS - 1):
                        scatter(s, b, i)
                    if i < IN and not (last and i == IN - 1):
                        add_state(b, i, 1)
                    if i == 3 and prev is not None:
                        finish(prev)
                        add_out(prev, s + 1, prev + 1)

                pool.wait_ge(s_brow, 48)
                pool.wait_ge(s_const2, 48)
                n = [0]

                def link(ins):
                    n[0] += 1
                    ins.then_inc(s_pb, 1)
                    pool.wait_ge(s_pb, n[0])

                for r in range(3):
                    rows_e = stage1[32 * r:32 * r + E, :]
                    link(pool.tensor_tensor(rows_e, rows_e, rowb[32 * r:32 * r + E, 0:D], ALU.add))
                for part, (st_, lo, hi) in enumerate(((stage0, 0, H), (stage1, H, BW))):
                    bp = bpart[:, lo:hi]
                    link(pool.tensor_copy(bp, st_))
                    link(pool.tensor_tensor(st_, st_, bp, ALU.subtract))
                    link(pool.tensor_copy(bp[32:64, :], st_[32:64, :]))
                    link(pool.tensor_copy(bp[64:96, :], st_[64:96, :]))
                    pool.tensor_tensor(bp[64:96, :], st_[64:96, :], bp[64:96, :], ALU.subtract).then_inc(s_brd, 1)
                    pool.wait_ge(s_brd, part + 1)

                def weights_in(i, q, first=False):
                    placed, rows_in = held(pool, i * 2 + q - 1), held(pool, i * 2 + q + 1)
                    pool.wait_ge(s_val, 1)
                    if not first:
                        pool.wait_ge(s_idm, placed)
                    pool.wait_ge(s_oa, rows_in)
                    if q == 1:
                        pool.tensor_tensor(ov[q][:, :, 0, :], oa[q],
                                           idv[:, bass.ts(i * 2 + q, CH)].unsqueeze(2).to_broadcast([P, CH, MC]),
                                           ALU.mult).then_inc(s_oi[1], 1)
                    pool.tensor_tensor(ov[q][:, :, 1, :], oa[q],
                                       wv[:, bass.ts(i * 2 + q, CH)].unsqueeze(2).to_broadcast([P, CH, MC]),
                                       ALU.mult).then_inc(s_ov, 1)

                weights_in(0, 0, True)
                weights_in(0, 1, True)
                with pool.Fori(1, NCH // 2) as i:
                    weights_in(i, 0)
                    weights_in(i, 1)

                pool.wait_ge(s_acc, 16 * B)
                pool.wait_ge(s_tab, 2)
                for j in range(3):
                    gather(j)
                for i in range(4):
                    step(0, i)
                with pool.Fori(0, B - 1) as b:
                    for i in range(4, STEPS):
                        step(b, i)
                    for i in range(4):
                        step(b + 1, i, prev=b)
                for i in range(4, STEPS):
                    step(B - 1, i, last=True)
                add_out(B - 1, MT, B - 1 + TB)
                pool.wait_ge(s_xg, 16 * MT)
                pool.wait_ge(s_sct, 16 * MT)
                pool.wait_ge(s_acc, 16 * 2 * B)

            @block.scalar
            def _(act):
                act.activation(aneg, aneg, ACT.Exp).then_inc(s_an, 1)

                def conv_in(b, m, f):
                    act.wait_ge(s_frdy, f + 1)
                    if positive(b):
                        act.wait_ge(s_dtt, b)
                    act.activation(xsv[:, m, :], psum["fr"][:, :], ACT.Identity,
                                   bias=col[:, C_INB + m:C_INB + m + 1]).then_inc(s_ffree, 1)
                    if positive(b):
                        act.wait_ge(s_u, b)
                    else:
                        act.wait_ge(s_an0, 1)
                    act.wait_ge(s_ffree, f + 1)
                    w = C_CW + TAPS * m
                    act.activation(xc[:, m, :], xs[:, m, 0:L], ACT.Identity, scale=col[:, w:w + 1],
                                   bias=col[:, C_CB + m:C_CB + m + 1]).then_inc(s_tap0, 1)

                def gate_in(b, m, f):
                    if positive(b) and m == 0:
                        act.wait_ge(s_yg, b)
                    act.wait_ge(s_frdy, f + 1)
                    act.activation(gs[:, m, :], psum["fr"][:, :], ACT.Identity,
                                   bias=col[:, C_INB + KD + m:C_INB + KD + m + 1]).then_inc(s_ffree, 1)
                    act.wait_ge(s_dtt, b + 1)
                    act.wait_ge(s_ffree, f + 1)
                    act.activation(sp[:, m, :], gs[:, m, :], ACT.Tanh, scale=0.5).then_inc(s_gt, 1)

                def conv_tanh(b):
                    for m in range(KD):
                        act.wait_ge(s_tap, (b + 1) * CT)
                        act.activation(xsv[:, m, :], xc[:, m, :], ACT.Tanh, scale=0.5).then_inc(s_ct, 1)

                def bc_in(b, f):
                    if positive(b):
                        act.wait_ge(s_gs, b * KD)
                    else:
                        act.wait_ge(s_dch, 1)
                        act.wait_ge(s_pb, 3)
                    act.wait_ge(s_frdy, f + 1)
                    if positive(b):
                        act.wait_ge(s_bcp, b)
                    act.activation(bcf, psum["fr"][0:PARTS, :], ACT.Identity,
                                   bias=col[0:PARTS, C_BCB:C_BCB + 1]).then_inc(s_bcf, 1)
                    act.activation(bcnext[:, :], psum["fr"][0:PARTS, :], ACT.Identity,
                                   bias=col[0:PARTS, C_BCB:C_BCB + 1]).then_inc(s_ffree, 1)

                def dt_in(b, m, f):
                    act.wait_ge(s_frdy, f + 1)
                    if m == 1:
                        act.wait_ge(s_part, b * 4 + 4)
                    act.activation(sp[:, m, :], psum["fr"][:, :], ACT.Abs,
                                   bias=col[:, C_DTB + m:C_DTB + m + 1]).then_inc(s_sp, 1)
                    act.activation(xsv[:, m, :], psum["fr"][:, :], ACT.Identity,
                                   bias=col[:, C_DTB + m:C_DTB + m + 1]).then_inc(s_ffree, 1)

                def exp_dt(b):
                    act.wait_ge(s_sp, b * 4 + 2)
                    act.activation(sp[:, :, :], sp[:, :, :], ACT.Exp, scale=-1.0).then_inc(s_sp, 1)

                def ln_dt(b):
                    act.wait_ge(s_sp, b * 4 + 3)
                    act.activation(sp[:, :, :], sp[:, :, :], ACT.Ln, bias=1.0).then_inc(s_sp, 1)
                    act.activation(scrap[:, :], col[:, 0:1], ACT.Exp)

                def start_sum(b):
                    if positive(b):
                        act.wait_ge(s_z1, b)
                    else:
                        act.wait_ge(s_tab, 2)
                    for m in range(KD):
                        act.activation(y[:, m, :], xc[:, m, :], ACT.Copy, scale=dhalf[:, m:m + 1]).then_inc(s_y0, 1)

                def decay(b, i, r):
                    g = b * NST + i * NU + r
                    if i == 0 and r == 0:
                        act.wait_ge(s_dtt, b + 1)
                    act.wait_ge(s_dafree, g + 1)
                    for k in range(KD):
                        n = i * NU + r
                        act.activation(da[:, r, k, 1:], dtt[:, k, 1:], ACT.Exp,
                                       scale=aneg[:, k, n:n + 1]).then_inc(s_da, 1)

                def copy_x(j):
                    act.wait_ge(s_xtr, j + 1)
                    if positive(j):
                        act.wait_ge(s_up, j * 2)
                    act.activation(xgt[:, :, :], tr_x.rearrange("p (k c) -> p k c", k=KD), ACT.Copy).then_inc(s_xtc, 1)

                def tanh_h(j, h):
                    act.wait_ge(s_up, j * 2 + h + 1)
                    if h == 0 and positive(j):
                        act.wait_ge(s_t, j * 2)
                    act.activation(th[:, h * 512:(h + 1) * 512], psum[f"up{h}"][:, :], ACT.Tanh,
                                   scale=0.5).then_inc(s_th, 1)

                def copy_h(j):
                    for h in range(2):
                        act.wait_ge(s_t, j * 2 + h + 1)
                        if h == 0 and positive(j):
                            act.wait_ge(s_dn, j)
                        act.activation(ht[:, 4 * h:4 * h + 4, :],
                                       psum[f"tr{h}"][:, :].rearrange("p (k c) -> p k c", c=P), ACT.Copy,
                                       scale=0.5).then_inc(s_ht, 1)

                def weigh(j):
                    act.wait_ge(s_dn, j + 1)
                    if positive(j):
                        act.wait_ge(s_sct, j * 16)
                    act.activation(yo[:, :], yx_y, ACT.Copy, scale=wslot[:, bass.ds(j, 1)]).then_inc(s_y, 1)

                def normalise(b):
                    act.wait_ge(s_nb, b + 1)
                    for j in range(TB):
                        act.activation(xtok[:, j, :], xtok[:, j, :], ACT.Identity, scale=rstd[:, j:j + 1],
                                       bias=rt_t[:, j:j + 1]).then_inc(s_zn, 1)

                def step(b, i, prev=None, last=False):
                    s, f = b * STEPS + i, b * FS
                    prepare = not last
                    if i < IN:
                        decay(b, i, 0)
                    if not (last and i == STEPS - 1):
                        copy_h(s)
                    if i == 8 and prepare:
                        ln_dt(b + 1)
                    if not (last and i >= STEPS - 2):
                        for h in range(2):
                            tanh_h(s + 1, h)
                    if i in (0, 1):
                        gate_in(b, i, f + F_G0 + i)
                    if i in (2, 3) and prepare:
                        conv_in(b + 1, i - 2, f + F_IN0 + i - 2)
                    if i == 4 and prepare:
                        conv_tanh(b + 1)
                    if i == 5 and prepare:
                        bc_in(b + 1, f + F_BC)
                    if i in (6, 7) and prepare:
                        dt_in(b + 1, i - 6, f + F_DT0 + i - 6)
                    if i < IN:
                        decay(b, i, 1)
                    if not (last and i >= STEPS - 3):
                        copy_x(s + 2)
                    if not (last and i == STEPS - 1):
                        weigh(s)
                    if i == 2 and prev is not None:
                        normalise(prev)
                    if i == 7 and prepare:
                        exp_dt(b + 1)
                    if i == 8 and prepare:
                        start_sum(b + 1)

                conv_in(0, 0, 0)
                conv_in(0, 1, 1)
                act.wait_ge(s_l, 1)
                act.activation(e2[:, 0:TT], l01[:, 0:TT], ACT.Exp).then_inc(s_e2, 1)
                conv_tanh(0)
                bc_in(0, 2)
                dt_in(0, 0, 3)
                dt_in(0, 1, 4)
                exp_dt(0)
                ln_dt(0)

                start_sum(0)
                copy_x(0)
                for h in range(2):
                    tanh_h(0, h)
                copy_x(1)
                act.wait_ge(s_an, 2)
                for i in range(2):
                    step(0, i)
                step(0, 2)
                with act.Fori(0, B - 2) as b:
                    for i in range(3, STEPS):
                        step(b, i)
                    for i in range(3):
                        step(b + 1, i, prev=b)
                for i in range(3, STEPS):
                    step(B - 2, i)
                for i in range(3):
                    step(B - 1, i, prev=B - 2, last=True)
                for i in range(3, STEPS):
                    step(B - 1, i, last=True)

            @block.vector
            def _(dve):
                dve.memset(xs[:, :, 0:TAPS - 1], 0.0).then_inc(s_an0, 1)
                dve.wait_ge(s_an, 1)
                dve.tensor_scalar(aneg, aneg, -1.0, None, ALU.mult).then_inc(s_an, 1)
                dve.wait_ge(s_an0, 1)

                def conv(b, m):
                    dve.wait_ge(s_tap0, b * KD + m + 1)
                    w = C_CW + TAPS * m
                    at = b * CT + (TAPS - 1) * m
                    for t in range(1, TAPS):
                        if t > 1:
                            dve.wait_ge(s_tap, at + t - 1)
                        dve.scalar_tensor_tensor(xc[:, m, :], xs[:, m, t:t + L], col[:, w + t:w + t + 1], xc[:, m, :],
                                                 ALU.mult, ALU.add).then_inc(s_tap, 1)

                def gate(b, m):
                    dve.wait_ge(s_gt, b * KD + m + 1)
                    dve.scalar_tensor_tensor(gs[:, m, :], sp[:, m, :], 1.0, gs[:, m, :], ALU.add,
                                             ALU.mult).then_inc(s_gs, 1)

                def conv_act(b):
                    for m in range(KD):
                        dve.wait_ge(s_ct, b * KD + m + 1)
                        dve.scalar_tensor_tensor(xc[:, m, :], xsv[:, m, :], 1.0, xc[:, m, :], ALU.add,
                                                 ALU.mult).then_inc(s_xv, 1)

                def bc_parts(b, f):
                    dve.wait_ge(s_bcf, b + 1)
                    dve.wait_ge(s_ffree, f + 1)
                    dve.tensor_tensor(bcf, bcf, bcnext[:, :], ALU.subtract).then_inc(s_part, 1)
                    dve.wait_ge(s_part, b * 4 + 1)
                    for r in (1, 2):
                        dve.tensor_copy(bcnext[32 * r:32 * r + 32, :], bcf[32 * r:32 * r + 32, :]).then_inc(s_part, 1)
                    dve.wait_ge(s_part, b * 4 + 3)
                    dve.tensor_tensor(bcnext[64:96, :], bcf[64:96, :], bcnext[64:96, :], ALU.subtract).then_inc(s_part, 1)

                def take_bc(b):
                    if positive(b):
                        dve.wait_ge(s_bcr, b * NST)
                    dve.wait_ge(s_part, b * 4 + 4)
                    dve.tensor_copy(bcpart[:, :], bcnext[:, :]).then_inc(s_bcp, 1)

                def inputs(b):
                    if positive(b):
                        dve.wait_ge(s_da, b * NST * KD)
                    dve.wait_ge(s_sp, b * 4 + 4)
                    dve.scalar_tensor_tensor(dtt[:, :, :], xsv, 0.0, sp[:, :, :], ALU.max, ALU.add).then_inc(s_dtt, 1)
                    dve.wait_ge(s_dtt, b + 1)
                    dve.scalar_tensor_tensor(u[:, :, :], xc, 0.5, dtt[:, :, :], ALU.mult, ALU.mult).then_inc(s_u, 1)

                def hidden(j, h):
                    dve.wait_ge(s_th, j * 2 + h + 1)
                    dve.scalar_tensor_tensor(th[:, h * 512:(h + 1) * 512], th[:, h * 512:(h + 1) * 512], 1.0,
                                             psum[f"up{h}"][:, :], ALU.add, ALU.mult).then_inc(s_hs, 1)

                def times_b(b, i, r):
                    g = b * NST + i * NU + r
                    if i == 0 and r == 0:
                        dve.wait_ge(s_u, b + 1)
                    dve.wait_ge(s_bb, g + 1)
                    if positive(g - 1):
                        dve.wait_ge(s_sum, g - 1)
                    dve.tensor_tensor(ring[:, r, :, :], u[:, :, :],
                                      psum["bb"][:, :].unsqueeze(1).to_broadcast([P, KD, L]),
                                      ALU.mult).then_inc(s_um, 1)

                def scan_c(b, i, r):
                    g = b * NST + i * NU + r
                    row = ring[:, r, :, :]
                    dve.wait_ge(s_um, g + 1)
                    dve.wait_ge(s_da, g * 2 + 2)
                    dve.tensor_tensor_scan(row.rearrange("p k l -> p (k l)"),
                                           da[:, r, :, :].rearrange("p k l -> p (k l)"),
                                           row.rearrange("p k l -> p (k l)"), 0.0, ALU.mult,
                                           ALU.add).then_inc(s_dafree, 1)
                    dve.wait_ge(s_dafree, g + 3)
                    dve.wait_ge(s_bcr, g + 1)
                    dve.tensor_tensor(row, row, psum["bc"][:, :].unsqueeze(1).to_broadcast([P, KD, L]),
                                      ALU.mult).then_inc(s_hc, 1)

                def gated(b):
                    dve.wait_ge(s_sum, (b + 1) * NST)
                    dve.wait_ge(s_gs, (b + 1) * KD)
                    dve.scalar_tensor_tensor(y[:, :, :], y[:, :, :], 0.5, gs[:, :, :], ALU.mult,
                                             ALU.mult).then_inc(s_yg, 1)

                def add_xn(b, f):
                    dve.wait_ge(s_xtok, b * 16 + 16)
                    dve.wait_ge(s_frdy, f + 1)
                    dve.tensor_tensor(xtok[:, 0:2, :], xtok[:, 0:2, :],
                                      psum["fr"][:, :].rearrange("p (j d) -> p j d", j=2), ALU.add).then_inc(s_ffree, 1)
                    dve.wait_ge(s_o1, b + 1)
                    dve.tensor_tensor(xtok[:, 2:4, :], xtok[:, 2:4, :],
                                      psum["bc"][:, :].rearrange("p (j d) -> p j d", j=2), ALU.add).then_inc(s_z1, 1)

                def statistics(b, f):
                    dve.wait_ge(s_ffree, f + 1)
                    dve.wait_ge(s_z1, b + 1)
                    for j in range(TB):
                        dve.bn_stats(stat[:, j, :], xtok[:, j, :]).then_inc(s_zs, 1)
                    counted = held(dve, b * TB + TB)
                    dve.wait_ge(s_an, 2)
                    dve.wait_ge(s_zs, counted)
                    for j in range(TB):
                        dve.bn_aggr(mv[:, j, :], stat[:, j, :]).then_inc(s_za, 1)

                def invert(b):
                    dve.wait_ge(s_za, b * TB + TB)
                    rsqrt(dve, rstd[:, :], mv[:, :, 1], rt_i[:, :], rt_t[:, :], s_zr, b * RSQ)
                    dve.scalar_tensor_tensor(rt_t[:, :], mv[:, :, 0], -1.0, rstd[:, :], ALU.mult,
                                             ALU.mult).then_inc(s_nb, 1)

                def step(b, i, prev=None, last=False):
                    s, f = b * STEPS + i, b * FS
                    prepare = not last
                    if i < IN:
                        times_b(b, i, 0)
                        scan_c(b, i, 0)
                        if not (last and i >= STEPS - 2):
                            hidden(s + 1, 0)
                            hidden(s + 1, 1)
                        times_b(b, i, 1)
                        scan_c(b, i, 1)
                    if i in (0, 1):
                        gate(b, i)
                    if prev is not None:
                        if i == 0:
                            statistics(prev, prev * FS + F_OUT)
                        if i == 1:
                            invert(prev)
                    if i in (2, 3) and prepare:
                        conv(b + 1, i - 2)
                    if i == 4 and prepare:
                        conv_act(b + 1)
                    if i == 5 and prepare:
                        bc_parts(b + 1, f + F_BC)
                    if i == 8 and prepare:
                        take_bc(b + 1)
                        inputs(b + 1)
                        gated(b)
                        hidden(s + 1, 0)
                        hidden(s + 1, 1)
                        add_xn(b, f + F_OUT)

                steps = [0]

                def link(ins):
                    steps[0] += 1
                    ins.then_inc(s_dch, 1)
                    dve.wait_ge(s_dch, steps[0])

                dve.wait_ge(s_k2, 32)
                dve.wait_ge(s_const2, 48)
                link(dve.tensor_tensor(lg, logit.rearrange("p t e -> p e t"),
                                       rowb[:, D:D + E].unsqueeze(2).to_broadcast([P, E, TT]), ALU.add))
                link(dve.memset(rank, 0.0))
                for j in range(E):
                    one = lg[:, j:j + 1, :]
                    if j > 0:
                        dve.tensor_tensor(beats[:, 0:j, :], one.to_broadcast([P, j, TT]), lg[:, 0:j, :], ALU.is_gt).then_inc(s_l2, 1)
                    if j < E - 1:
                        dve.tensor_tensor(beats[:, j + 1:E, :], one.to_broadcast([P, E - 1 - j, TT]),
                                          lg[:, j + 1:E, :], ALU.is_ge).then_inc(s_l2, 1)
                    if 0 < j < E - 1:
                        dve.wait_ge(s_l2, 2 * j + 1)
                        link(dve.memset(beats[:, j, :], 0.0))
                        link(dve.tensor_tensor(rank, rank, beats, ALU.add))
                    elif j == 0:
                        dve.wait_ge(s_l2, 1)
                        link(dve.tensor_tensor(rank[:, 1:E, :], rank[:, 1:E, :], beats[:, 1:E, :], ALU.add))
                    else:
                        dve.wait_ge(s_l2, 2 * j)
                        link(dve.tensor_tensor(rank[:, 0:j, :], rank[:, 0:j, :], beats[:, 0:j, :], ALU.add))
                dve.tensor_scalar(both.rearrange("p (e t) -> p e t", e=E), rank, float(TOPK), None,
                                  ALU.is_lt).then_inc(s_both, 1)
                for k, top in enumerate((top0, top1)):
                    link(dve.tensor_scalar(top, rank, float(k), None, ALU.is_equal))
                    link(dve.tensor_tensor(tmp, top, lg, ALU.mult))
                    link(dve.tensor_reduce(af[:, k * TT:(k + 1) * TT], tmp.rearrange("p e t -> p t e"), AX.X, ALU.add))
                dve.tensor_tensor(l01[:, 0:TT], af[:, TT:2 * TT], af[:, 0:TT], ALU.subtract).then_inc(s_l, 1)
                conv(0, 0)
                conv(0, 1)
                dve.wait_ge(s_cum, 2)
                tot = psum["bc"][:, 0:256]
                link(dve.tensor_tensor_scan(incl.rearrange("p e t -> p (e t)"), k_rst, tot, 0.0, ALU.mult, ALU.add))
                link(dve.tensor_tensor(slot, incl, tot.rearrange("p (e t) -> p e t", e=E), ALU.subtract))
                link(dve.tensor_copy(cnt, incl[:, :, TT - 1]))
                link(dve.tensor_tensor(tmp, cnt.unsqueeze(2).to_broadcast([P, E, TT]),
                                       k_128.unsqueeze(1).to_broadcast([P, E, TT]), ALU.is_gt))
                link(dve.tensor_reduce(nt, tmp, AX.X, ALU.add))
                link(dve.memset(unit, 1.0))
                link(dve.tensor_tensor_scan(sinc, unit, nt, 0.0, ALU.mult, ALU.add))
                link(dve.tensor_tensor(st, sinc, nt, ALU.subtract))
                link(dve.tensor_scalar(st128, st, float(P), None, ALU.mult))
                link(dve.tensor_tensor(slot, slot, psum["bb"][:, 0:256].rearrange("p (e t) -> p e t", e=E), ALU.add))
                link(dve.tensor_tensor(slot, slot, st128.unsqueeze(2).to_broadcast([P, E, TT]), ALU.add))
                for k, top in enumerate((top0, top1)):
                    link(dve.tensor_tensor(tmp, top, slot, ALU.mult))
                    link(dve.tensor_reduce(slotf[:, k * TT:(k + 1) * TT], tmp.rearrange("p e t -> p t e"), AX.X, ALU.add))
                link(dve.tensor_copy(sloti, slotf))
                link(dve.tensor_single_scalar(ai, sloti, 7, ALU.logical_shift_right))
                link(dve.tensor_single_scalar(bi, sloti, P - 1, ALU.bitwise_and))
                link(dve.tensor_copy(af, ai))
                link(dve.tensor_copy(bf, bi))
                link(dve.tensor_tensor(idv.rearrange("p (k t) -> p k t", k=TOPK),
                                       k_tok.unsqueeze(1).to_broadcast([P, TOPK, TT]),
                                       bf.rearrange("p (k t) -> p k t", k=TOPK), ALU.subtract))
                dve.wait_ge(s_e2, 1)
                link(dve.tensor_scalar(l01[:, TT:2 * TT], e2[:, 0:TT], 1.0, None, ALU.add))
                link(dve.reciprocal(wv[:, 0:TT], l01[:, TT:2 * TT]))
                dve.tensor_tensor(wv[:, TT:2 * TT], e2[:, 0:TT], wv[:, 0:TT], ALU.mult).then_inc(s_val, 1)

                def one_hot(i, q, first=False):
                    if not first:
                        dve.wait_ge(s_ov, i * 2 + q - 1)
                        dve.wait_ge(s_oi[q], i)
                    dve.tensor_tensor(oa[q], k_j.unsqueeze(1).to_broadcast([P, CH, MC]),
                                      af[:, bass.ts(i * 2 + q, CH)].unsqueeze(2).to_broadcast([P, CH, MC]),
                                      ALU.is_equal).then_inc(s_oa, 1)
                    if not first:
                        dve.wait_ge(s_idm, i * 2 + q - 1)
                    dve.tensor_tensor(ob[q], k_iota.unsqueeze(1).to_broadcast([P, CH, P]),
                                      bf[:, bass.ts(i * 2 + q, CH)].unsqueeze(2).to_broadcast([P, CH, P]),
                                      ALU.is_equal).then_inc(s_ob, 1)
                    if q == 0:
                        dve.wait_ge(s_oa, i * 2 + 1)
                        dve.tensor_tensor(ov[q][:, :, 0, :], oa[q],
                                          idv[:, bass.ts(i * 2, CH)].unsqueeze(2).to_broadcast([P, CH, MC]),
                                          ALU.mult).then_inc(s_oi[0], 1)

                conv_act(0)
                for q in range(2):
                    dve.wait_ge(s_xnw[q], 16 * B // 2)
                one_hot(0, 0, True)
                one_hot(0, 1, True)
                bc_parts(0, 2)
                take_bc(0)
                with dve.Fori(1, NCH // 2) as i:
                    one_hot(i, 0)
                    one_hot(i, 1)
                big = nslot_big.rearrange("p (c e) -> p c e", e=E)
                link(dve.tensor_tensor(big, st.unsqueeze(1).to_broadcast([P, MC, E]),
                                       k_j.unsqueeze(2).to_broadcast([P, MC, E]), ALU.is_le))
                link(dve.tensor_reduce(wslot[:, :], big, AX.X, ALU.add))
                link(dve.tensor_scalar(te_i[:, :], wslot[:, :], -1.0, None, ALU.add))
                dve.wait_ge(s_idm, NCH)
                ids = psum["up0"][:, 0:MC]
                link(dve.tensor_scalar(sid[:, :], ids, k_pad, None, ALU.add))
                dve.tensor_copy(wslot[:, :], psum["up0"][:, MC:2 * MC]).then_inc(s_tab, 1)
                dve.tensor_scalar(gid[:, :], ids, k_pad, float(TOK - 1), ALU.add, ALU.min).then_inc(s_tab, 1)

                for r in range(2):
                    dve.memset(da[:, r, :, 0], 0.0).then_inc(s_dafree, 1)
                inputs(0)
                for h in range(2):
                    hidden(0, h)
                for i in range(2):
                    step(0, i)
                with dve.Fori(0, B - 1) as b:
                    for i in range(2, STEPS):
                        step(b, i)
                    for i in range(2):
                        step(b + 1, i, prev=b)
                for i in range(2, STEPS - 1):
                    step(B - 1, i, last=True)
                dve.wait_ge(s_hc, B * NST)
                dve.wait_ge(s_sum, B * NST - 1)
                dve.tensor_tensor(y[:, :, :], y[:, :, :], ring[:, 1, :, :], ALU.add).then_inc(s_sum, 1)
                gated(B - 1)
                add_xn(B - 1, (B - 1) * FS + F_OUT_LAST)
                statistics(B - 1, (B - 1) * FS + F_OUT_LAST)
                invert(B - 1)
                for j in range(TB):
                    dve.tensor_scalar(xtok[:, j, :], xtok[:, j, :], mv[:, j, 0:1], rstd[:, j:j + 1],
                                      ALU.subtract, ALU.mult).then_inc(s_zn, 1)
                for j in range(TB):
                    dve.wait_ge(s_zn, (B - 1) * TB + j + 1)
                    dve.tensor_tensor(xtok[:, j, :], xtok[:, j, :], gam[:, :], ALU.mult).then_inc(s_zg, 1)

            @block.tensor
            def _(pe):
                def project(at, rows_out, f, src):
                    if positive(f):
                        pe.wait_ge(s_ffree, f)
                    for k in range(KD):
                        mm = pe.matmul(psum["fr"][0:rows_out, :], wm[:, k, at:at + rows_out], src[:, k, :],
                                       start=(k == 0), stop=(k == KD - 1))
                    mm.then_inc(s_frdy, 1)

                def proj_in(b, m, f):
                    if m == 0:
                        pe.wait_ge(s_xnt, b * 16 + 16)
                    project(W_IN + m * P, P, f, xnt)

                def proj_bc(b, f):
                    pe.wait_ge(s_xv, b * KD + KD)
                    project(W_BC, PARTS, f, xc)

                def proj_dt(m, f):
                    project(W_DT + m * P, P, f, xc)

                def proj_out(b, f):
                    pe.wait_ge(s_yg, b + 1)
                    pe.wait_ge(s_ffree, f)
                    for o, (bank, ready) in enumerate((("fr", s_frdy), ("bc", s_o1))):
                        for c in range(2):
                            j = 2 * o + c
                            dst = psum[bank][:, c * D:(c + 1) * D]
                            pe.matmul(dst, sel[:, E:E + 1].to_broadcast([PARTS, P]), bpart[:, H:BW],
                                      start=True, stop=False)
                            for k in range(KD):
                                mm = pe.matmul(dst, y[:, k, j * P:(j + 1) * P], wm[:, k, W_OUT:W_OUT + D],
                                               start=False, stop=(k == KD - 1))
                        mm.then_inc(ready, 1)

                def spread_b(b, i, r):
                    g, n = b * NST + i * NU + r, i * NU + r
                    if i == 0 and r == 0:
                        pe.wait_ge(s_bcp, b + 1)
                    if positive(g):
                        pe.wait_ge(s_um, g)
                    pe.matmul(psum["bb"][:, :], sel[:, n:n + 1].to_broadcast([PARTS, P]), bcpart[:, :],
                              start=True, stop=True).then_inc(s_bb, 1)

                def spread_c(b, i, r):
                    g, n = b * NST + i * NU + r, i * NU + r + NST
                    if positive(g):
                        pe.wait_ge(s_hc, g)
                        if i == 0 and r == 0:
                            pe.wait_ge(s_z1, b)
                    pe.matmul(psum["bc"][:, :], sel[:, n:n + 1].to_broadcast([PARTS, P]), bcpart[:, :],
                              start=True, stop=True).then_inc(s_bcr, 1)

                def turn_x(j):
                    pe.wait_ge(s_xg, j * 16 + 16)
                    if positive(j - 1):
                        pe.wait_ge(s_ht, j * 2 - 2)
                    for k in range(KD):
                        mm = pe.transpose(tr_x[:, k * P:(k + 1) * P], xg[:, k * P:(k + 1) * P], ident[:, :])
                    mm.then_inc(s_xtr, 1)

                def expert(j):
                    return pe.value_load(te_i[0:1, bass.ds(j, 1)], min_val=0, max_val=E - 1)

                def up(j, e, h):
                    if h == 0:
                        pe.wait_ge(s_xtc, j + 1)
                        if positive(j):
                            pe.wait_ge(s_hs, j * 2)
                    cs = slice(h * 512, (h + 1) * 512)
                    pe.matmul(psum[f"up{h}"][:, :], sel[:, bass.ds(e, 1)].to_broadcast([PARTS, P]), bpart[:, cs],
                              start=True, stop=False)
                    for k in range(KD):
                        mm = pe.matmul(psum[f"up{h}"][:, :], xgt[:, k, :], w1[:, bass.ds(e, 1), k, cs],
                                       start=False, stop=(k == KD - 1))
                    mm.then_inc(s_up, 1)

                def turn_h(j, followed=True):
                    for h in range(2):
                        if h == 0 and positive(j):
                            pe.wait_ge(s_ht, j * 2)
                        if h == 1 and followed:
                            pe.wait_ge(s_xtc, j + 2)
                        pe.wait_ge(s_hs, j * 2 + h + 1)
                        for c in range(4):
                            at = (4 * h + c) * P
                            mm = pe.transpose(psum[f"tr{h}"][:, c * P:(c + 1) * P], th[:, at:at + P], ident[:, :])
                        mm.then_inc(s_t, 1)

                def down(j, e, half):
                    if half == 0:
                        pe.wait_ge(s_ht, j * 2 + 2)
                        if positive(j):
                            pe.wait_ge(s_y, j)
                        pe.matmul(yx_y, sel[:, bass.ds(e, 1)].to_broadcast([PARTS, P]), bpart[:, H:BW],
                                  start=True, stop=False)
                    for k in range(half * KH // 2, (half + 1) * KH // 2):
                        mm = pe.matmul(yx_y, ht[:, k, :], w2[:, bass.ds(e, 1), k, :], start=False, stop=(k == KH - 1))
                    if half == 1:
                        mm.then_inc(s_dn, 1)

                def step(b, i, e, e_next, last=False):
                    s, f = b * STEPS + i, b * FS
                    prepare = not last
                    first_layer = not (last and i >= STEPS - 2)
                    second_layer = not (last and i == STEPS - 1)
                    if i < IN:
                        spread_b(b, i, 0)
                    if first_layer:
                        up(s + 1, e_next, 0)
                    if i < IN:
                        spread_c(b, i, 0)
                    if i in (0, 1):
                        proj_in(b, KD + i, f + F_G0 + i)
                    if i in (2, 3) and prepare:
                        proj_in(b + 1, i - 2, f + F_IN0 + i - 2)
                    if i in (6, 7) and prepare:
                        proj_dt(i - 6, f + F_DT0 + i - 6)
                    if first_layer:
                        up(s + 1, e_next, 1)
                    e_after = None if last and i >= STEPS - 3 else expert(s + 2)
                    if i == 5 and prepare:
                        proj_bc(b + 1, f + F_BC)
                    if second_layer:
                        down(s, e, 0)
                    if i < IN:
                        spread_b(b, i, 1)
                    if second_layer:
                        if not (last and i >= STEPS - 3):
                            turn_x(s + 2)
                        down(s, e, 1)
                    if i < IN:
                        spread_c(b, i, 1)
                    if i == 8:
                        proj_out(b, f + (F_OUT_LAST if last else F_OUT))
                    if first_layer:
                        turn_h(s + 1, followed=not (last and i >= STEPS - 3))
                    return e_next, e_after

                proj_in(0, 0, 0)
                proj_in(0, 1, 1)
                pe.wait_ge(s_both, 1)
                pe.matmul(psum["bb"][:, 0:256], tri, both, start=True, stop=True).then_inc(s_cum, 1)
                pe.matmul(psum["bc"][:, 0:256], ones, both, start=True, stop=True).then_inc(s_cum, 1)

                def place(i, q, a, first, last):
                    return pe.matmul(psum["up0"][:, 0:2 * MC], ob[q][:, a, :],
                                     ov[q][:, a, :, :].rearrange("p v c -> p (v c)"), start=first, stop=last)

                def chunk(i, q, first, last):
                    pe.wait_ge(s_ob, i * 2 + q + 1)
                    pe.wait_ge(s_oi[q], i + 1)
                    pe.wait_ge(s_ov, i * 2 + q + 1)
                    for a in range(CH):
                        mm = place(i, q, a, first and a == 0, last and a == CH - 1)
                    mm.then_inc(s_idm, 1)

                proj_bc(0, 2)
                chunk(0, 0, True, False)
                proj_dt(0, 3)
                chunk(0, 1, False, False)
                proj_dt(1, 4)
                with pe.Fori(1, NCH // 2 - 1) as i:
                    chunk(i, 0, False, False)
                    chunk(i, 1, False, False)
                chunk(NCH // 2 - 1, 0, False, False)
                chunk(NCH // 2 - 1, 1, False, True)

                turn_x(0)
                pe.wait_ge(s_tab, 2)
                e = expert(0)
                pe.wait_ge(s_brd, 2)
                pe.wait_ge(s_w, 16 * 2 * E)
                for h in range(2):
                    up(0, e, h)
                turn_x(1)
                turn_h(0)
                e_next = expert(1)
                for i in range(2):
                    e, e_next = step(0, i, e, e_next)
                with pe.Fori(0, B - 1) as b:
                    e, e_next = expert(b * STEPS + 2), expert(b * STEPS + 3)
                    for i in range(2, STEPS):
                        e, e_next = step(b, i, e, e_next)
                    for i in range(2):
                        e, e_next = step(b + 1, i, e, e_next)
                e, e_next = expert((B - 1) * STEPS + 2), expert((B - 1) * STEPS + 3)
                for i in range(2, STEPS):
                    e, e_next = step(B - 1, i, e, e_next, last=True)
    return nc


_ORDER = ("x", "cols", "rows", "wmix", "wroute", "brows", "we1", "we2", "consts", "constb")


def kernel(**inputs):
    import ml_dtypes
    import numpy as np
    import concourse.bacc as bacc
    from concourse.bass_utils import run_bass_kernel_spmd

    a = {k[3:]: np.asarray(v) for k, v in inputs.items()}

    def by_part(v):
        return v.reshape(-1, P).T

    def rows_of(w):
        return w.reshape(KD, P, -1).transpose(1, 0, 2)

    bcb = np.concatenate([a["attn_bc_b"]] * 3 + [np.zeros(P - PARTS, np.float32)])
    bcw = a["attn_bc_w"].T
    brows = np.zeros((32, BW), np.float32)
    brows[0:E, 0:H] = a["ffn_be1"]
    brows[0:E, H:BW] = a["ffn_be2"]
    brows[E, H:BW] = a["attn_out_b"]
    lay = {
        "x": a["attn_x"].reshape(TOK, D),
        "cols": np.concatenate([by_part(a["attn_in_proj_b"]), a["attn_conv_w"].reshape(KD, P, TAPS).transpose(1, 0, 2).reshape(P, -1),
                                by_part(a["attn_conv_b"]), by_part(a["attn_dt_b"]), by_part(a["attn_D"]),
                                a["attn_A_log"].reshape(KD, P, NST).transpose(1, 0, 2).reshape(P, -1),
                                by_part(a["ffn_rb1"]), by_part(bcb)], axis=1),
        "rows": np.concatenate([a["attn_ln_g"], a["attn_ln_b"], a["ffn_rb2"]]),
        "wmix": rows_of(np.concatenate([a["attn_in_proj_w"].T, bcw, bcw, bcw, a["attn_dt_w"].T, a["attn_out_w"].T], axis=1)),
        "wroute": rows_of(np.concatenate([a["ffn_rw1"], a["ffn_rw2"]], axis=1)),
        "brows": brows,
        "we1": a["ffn_we1"],
        "we2": a["ffn_we2"],
    }
    p = np.arange(P, dtype=np.float32)
    one = np.ones((P, 1), np.float32)
    reset = (np.arange(E * TT) % TT != 0).astype(np.float32)
    lay["consts"] = np.concatenate([
        np.eye(P, dtype=np.float32), one * p, one * np.arange(MC, dtype=np.float32),
        one * (P * np.arange(TT, dtype=np.float32)), one * reset,
        p[:, None] + P * np.arange(TT, dtype=np.float32) - TOK, p[:, None] + TOK], axis=1)
    lay["constb"] = np.concatenate([p[:, None] < p, np.ones((P, P), bool), p[:, None] % 32 == np.arange(32)],
                                   axis=1).astype(ml_dtypes.bfloat16)

    nc = bacc.Bacc("TRN2", target_bir_lowering=False, num_devices=1)
    arrays, args = {}, []
    for name in _ORDER:
        v = np.ascontiguousarray(lay[name])
        arrays[f"in_{name}"] = v
        args.append(nc.dram_tensor(f"in_{name}", v.shape, mybir.dt.from_np(v.dtype), kind="ExternalInput").ap())
    res = nc.dram_tensor("out_0", (TOK, D), F32, kind="ExternalOutput").ap()
    build(nc, *args, res)
    r = run_bass_kernel_spmd(nc, [arrays], core_ids=[0])
    return r.results[0]["out_0"].reshape(B, L, D)
```
